# Optimizing a Trainium2 kernel written in Bass

```python
import numpy as np
import jax
import jax.numpy as jnp

def _softmax(x, axis=-1):
    return jax.nn.softmax(x, axis=axis)

def _gelu(x):
    return jax.nn.gelu(x, approximate=True)

def _silu(x):
    return jax.nn.silu(x)

def _sigmoid(x):
    return jax.nn.sigmoid(x)

def _layernorm(x, axis=-1, eps=1e-05):
    m = jnp.mean(x, axis=axis, keepdims=True)
    v = jnp.var(x, axis=axis, keepdims=True)
    return (x - m) / jnp.sqrt(v + eps)

def _scatter_add(tgt, idx, src, axis=0):
    return tgt.at[idx].add(src)

def _segment_sum(src, seg, n):
    return jax.ops.segment_sum(src, seg, n)
kernel_name = 'mk_macaron_d1_jaxref_r8_31ad0c'

def setup_inputs(seed: int=0):
    np.random.seed(seed)
    _w = jnp.asarray

    def _L0_attn_setup():
        import jax, jax.numpy as jnp
        import numpy as np
        DIM = 256
        N_HEADS = 32
        N_KV_HEADS = 8
        HEAD_DIM = 64
        REPEATS = N_HEADS // N_KV_HEADS
        SLIDING_WINDOW = 128
        EPS = 1e-06
        B, T = (2, 256)

        def _alibi_slopes(n):
            r = 2.0 ** (-8.0 / n)
            return jnp.asarray([r ** i for i in range(n)], dtype=jnp.float32)

        def _rms_norm(x, w, eps):
            var = jnp.mean(x * x, axis=-1, keepdims=True)
            return x * jax.lax.rsqrt(var + eps) * w
        key = jax.random.key(seed)
        ks = jax.random.split(key, 6)
        s = 0.02
        return {'x': jax.random.normal(ks[0], (B, T, DIM), jnp.float32), 'wq': jax.random.normal(ks[1], (N_HEADS * HEAD_DIM, DIM), jnp.float32) * s, 'wk': jax.random.normal(ks[2], (N_KV_HEADS * HEAD_DIM, DIM), jnp.float32) * s, 'wv': jax.random.normal(ks[3], (N_KV_HEADS * HEAD_DIM, DIM), jnp.float32) * s, 'wo': jax.random.normal(ks[4], (DIM, N_HEADS * HEAD_DIM), jnp.float32) * s, 'q_norm_w': jnp.ones((N_HEADS * HEAD_DIM,), jnp.float32), 'k_norm_w': jnp.ones((N_KV_HEADS * HEAD_DIM,), jnp.float32)}
    _L0_attn_in = _L0_attn_setup()

    def _L0_ffn_setup():
        import jax, jax.numpy as jnp
        import numpy as np
        HIDDEN = 256
        FFN = 176
        N_EXPERTS = 64
        TOP_K = 6
        N_SHARED = 2
        SHARED_FFN = FFN * N_SHARED
        ROUTED_SCALING = 1.0
        EPS = 1e-20

        def _moe_forward(x, gate_w, w_gate_up, w_down, ws_gate_up, ws_down):
            T = x.shape[0]
            logits = jnp.einsum('th,eh->te', x.astype(jnp.float32), gate_w.astype(jnp.float32))
            scores = jax.nn.softmax(logits, axis=-1)
            topk_w, topk_ids = jax.lax.top_k(scores, TOP_K)
            topk_w = topk_w / (jnp.sum(topk_w, axis=-1, keepdims=True) + EPS)
            topk_w = topk_w * ROUTED_SCALING
            comb = jnp.zeros((T, N_EXPERTS), dtype=x.dtype)
            comb = comb.at[jnp.arange(T)[:, None], topk_ids].add(topk_w.astype(x.dtype))
            gu = jnp.einsum('th,efh->tef', x, w_gate_up)
            g, u = (gu[..., :FFN], gu[..., FFN:])
            act = jax.nn.silu(g) * u
            act = act * comb[:, :, None]
            routed = jnp.einsum('tef,ehf->th', act, w_down)
            sgu = jnp.einsum('th,fh->tf', x, ws_gate_up)
            sg, su = (sgu[..., :SHARED_FFN], sgu[..., SHARED_FFN:])
            shared = jnp.einsum('tf,hf->th', jax.nn.silu(sg) * su, ws_down)
            return routed + shared
        key = jax.random.key(seed)
        k0, k1, k2, k3, k4, k5 = jax.random.split(key, 6)
        hidden_states = jax.random.normal(k0, (1, 32, HIDDEN), dtype=jnp.float32)
        gate_w = jax.random.normal(k1, (N_EXPERTS, HIDDEN), dtype=jnp.float32) * 0.05
        w_gate_up = jax.random.normal(k2, (N_EXPERTS, 2 * FFN, HIDDEN), dtype=jnp.float32) * 0.02
        w_down = jax.random.normal(k3, (N_EXPERTS, HIDDEN, FFN), dtype=jnp.float32) * 0.02
        ws_gate_up = jax.random.normal(k4, (2 * SHARED_FFN, HIDDEN), dtype=jnp.float32) * 0.02
        ws_down = jax.random.normal(k5, (HIDDEN, SHARED_FFN), dtype=jnp.float32) * 0.02
        return {'hidden_states': hidden_states, 'gate_w': gate_w, 'w_gate_up': w_gate_up, 'w_down': w_down, 'ws_gate_up': ws_gate_up, 'ws_down': ws_down}
    _L0_ffn_in = _L0_ffn_setup()
    _d = {'L0_attn_x': _L0_attn_in['x'], 'L0_attn_wq': _L0_attn_in['wq'], 'L0_attn_wk': _L0_attn_in['wk'], 'L0_attn_wv': _L0_attn_in['wv'], 'L0_attn_wo': _L0_attn_in['wo'], 'L0_attn_q_norm_w': _L0_attn_in['q_norm_w'], 'L0_attn_k_norm_w': _L0_attn_in['k_norm_w'], 'L0_ffn_gate_w': _L0_ffn_in['gate_w'], 'L0_ffn_w_gate_up': _L0_ffn_in['w_gate_up'], 'L0_ffn_w_down': _L0_ffn_in['w_down'], 'L0_ffn_ws_gate_up': _L0_ffn_in['ws_gate_up'], 'L0_ffn_ws_down': _L0_ffn_in['ws_down']}
    _x0 = _d['L0_attn_x']
    _d['L0_attn_x'] = jax.random.normal(jax.random.fold_in(jax.random.key(seed), 1), (2, 512, 256), dtype=_x0.dtype)
    del _x0
    return _d

def reference(L0_attn_x, L0_attn_wq, L0_attn_wk, L0_attn_wv, L0_attn_wo, L0_attn_q_norm_w, L0_attn_k_norm_w, L0_ffn_gate_w, L0_ffn_w_gate_up, L0_ffn_w_down, L0_ffn_ws_gate_up, L0_ffn_ws_down):

    def _L0_attn_ref(x, wq, wk, wv, wo, q_norm_w, k_norm_w):
        import jax, jax.numpy as jnp
        import numpy as np
        DIM = 256
        N_HEADS = 32
        N_KV_HEADS = 8
        HEAD_DIM = 64
        REPEATS = N_HEADS // N_KV_HEADS
        SLIDING_WINDOW = 128
        EPS = 1e-06
        B, T = (2, 256)

        def _alibi_slopes(n):
            r = 2.0 ** (-8.0 / n)
            return jnp.asarray([r ** i for i in range(n)], dtype=jnp.float32)

        def _rms_norm(x, w, eps):
            var = jnp.mean(x * x, axis=-1, keepdims=True)
            return x * jax.lax.rsqrt(var + eps) * w
        bsz, seqlen, _ = x.shape
        xq = _rms_norm(x @ wq.T, q_norm_w, EPS)
        xk = _rms_norm(x @ wk.T, k_norm_w, EPS)
        xv = x @ wv.T
        xq = xq.reshape(bsz, seqlen, N_HEADS, HEAD_DIM).transpose(0, 2, 1, 3)
        xk = xk.reshape(bsz, seqlen, N_KV_HEADS, HEAD_DIM).transpose(0, 2, 1, 3)
        xv = xv.reshape(bsz, seqlen, N_KV_HEADS, HEAD_DIM).transpose(0, 2, 1, 3)
        xk = jnp.repeat(xk, REPEATS, axis=1)
        xv = jnp.repeat(xv, REPEATS, axis=1)
        pos = jnp.arange(seqlen)
        dist = pos[None, :] - pos[:, None]
        slopes = _alibi_slopes(N_HEADS)
        alibi = slopes[:, None, None] * dist.astype(jnp.float32)
        allowed = (dist <= 0) & (dist >= -SLIDING_WINDOW)
        bias = jnp.where(allowed[None], alibi, -jnp.inf)
        scale = 1.0 / jnp.sqrt(jnp.asarray(HEAD_DIM, jnp.float32))
        scores = jnp.einsum('bhtd,bhsd->bhts', xq, xk) * scale + bias[None]
        attn = jax.nn.softmax(scores, axis=-1)
        out = jnp.einsum('bhts,bhsd->bhtd', attn, xv)
        out = out.transpose(0, 2, 1, 3).reshape(bsz, seqlen, N_HEADS * HEAD_DIM)
        return out @ wo.T

    def _L0_ffn_ref(hidden_states, gate_w, w_gate_up, w_down, ws_gate_up, ws_down):
        import jax, jax.numpy as jnp
        import numpy as np
        HIDDEN = 256
        FFN = 176
        N_EXPERTS = 64
        TOP_K = 6
        N_SHARED = 2
        SHARED_FFN = FFN * N_SHARED
        ROUTED_SCALING = 1.0
        EPS = 1e-20

        def _moe_forward(x, gate_w, w_gate_up, w_down, ws_gate_up, ws_down):
            T = x.shape[0]
            logits = jnp.einsum('th,eh->te', x.astype(jnp.float32), gate_w.astype(jnp.float32))
            scores = jax.nn.softmax(logits, axis=-1)
            topk_w, topk_ids = jax.lax.top_k(scores, TOP_K)
            topk_w = topk_w / (jnp.sum(topk_w, axis=-1, keepdims=True) + EPS)
            topk_w = topk_w * ROUTED_SCALING
            comb = jnp.zeros((T, N_EXPERTS), dtype=x.dtype)
            comb = comb.at[jnp.arange(T)[:, None], topk_ids].add(topk_w.astype(x.dtype))
            gu = jnp.einsum('th,efh->tef', x, w_gate_up)
            g, u = (gu[..., :FFN], gu[..., FFN:])
            act = jax.nn.silu(g) * u
            act = act * comb[:, :, None]
            routed = jnp.einsum('tef,ehf->th', act, w_down)
            sgu = jnp.einsum('th,fh->tf', x, ws_gate_up)
            sg, su = (sgu[..., :SHARED_FFN], sgu[..., SHARED_FFN:])
            shared = jnp.einsum('tf,hf->th', jax.nn.silu(sg) * su, ws_down)
            return routed + shared
        B, S, H = hidden_states.shape
        x = hidden_states.reshape(-1, H)
        out = _moe_forward(x, gate_w, w_gate_up, w_down, ws_gate_up, ws_down)
        return out.reshape(B, S, H)
    x = L0_attn_x
    x = x + 0.5 * _L0_ffn_ref(_layernorm(x, axis=-1), L0_ffn_gate_w, L0_ffn_w_gate_up, L0_ffn_w_down, L0_ffn_ws_gate_up, L0_ffn_ws_down)
    x = x + _L0_attn_ref(_layernorm(x, axis=-1), L0_attn_wq, L0_attn_wk, L0_attn_wv, L0_attn_wo, L0_attn_q_norm_w, L0_attn_k_norm_w)
    x = x + 0.5 * _L0_ffn_ref(_layernorm(x, axis=-1), L0_ffn_gate_w, L0_ffn_w_gate_up, L0_ffn_w_down, L0_ffn_ws_gate_up, L0_ffn_ws_down)
    return x

_drawn_inputs = setup_inputs


def setup_inputs(seed=0):
    import zlib

    import numpy as np

    out = dict(_drawn_inputs(seed))
    spreads = {'L0_attn_q_norm_w': (1.0, 0.6), 'L0_attn_k_norm_w': (1.0, 0.6)}
    factors = {'L0_ffn_gate_w': 8.0,
     'L0_ffn_w_gate_up': 8.0,
     'L0_ffn_w_down': 8.0,
     'L0_ffn_ws_gate_up': 2.85,
     'L0_ffn_ws_down': 2.846}
    for name, (base, spread) in spreads.items():
        noise = np.random.default_rng([zlib.crc32(name.encode()), seed]).standard_normal(out[name].shape)
        drawn = base * np.exp(spread * noise) if base else spread * noise
        out[name] = jnp.asarray(drawn.astype(out[name].dtype))
    for name, factor in factors.items():
        out[name] = (out[name] * factor).astype(out[name].dtype)
    return out
```

```python
from contextlib import ExitStack

import concourse.bass as bass
from concourse import mybir

F32 = mybir.dt.float32
BF16 = mybir.dt.bfloat16
I32 = mybir.dt.int32
U32 = mybir.dt.uint32
ALU = mybir.AluOpType
ACT = mybir.ActivationFunctionType
AX = mybir.AxisListType

P = 128
DIM = 256
KD = DIM // P
TOKENS = 1024
NT = TOKENS // P
BATCHES = 2
TB = NT // BATCHES
NE = 64
TOPK = 6
FFN = 176
FC = FFN // 2
RING = 4
ROW = DIM + 2
MAX_EXTRA = 48
MAX_BLOCKS = NE + MAX_EXTRA
NSH = 2 * NT
HEADS = 32
KVH = 8
HD = 64
REP = HEADS // KVH
QD = HEADS * HD
KVD = KVH * HD
QC = QD // P
KC = KVD // P
WINDOW = 128
MASKED = 1e34
PAIRS = TB * KVH * 2
LN_EPS, RMS_EPS, TOPK_EPS = 1e-5, 1e-6, 1e-20


def macaron(nc, x_in, gate_in, wgu_in, wdn_in, sgu_in, sdn_in, wq_in, wqn_in, wk_in, wkn_in,
            wv_in, wo_in, qn_in, kn_in, out):
    ctx = ExitStack()
    with ctx:
        def sb(name, shape, dt=F32):
            return ctx.enter_context(nc.sbuf_tensor(name, shape, dt))

        def sem(name):
            return ctx.enter_context(nc.semaphore(name))

        bank = [ctx.enter_context(nc.psum_tensor(f"bank{i}", [P, 512], F32)) for i in range(8)]

        routed = [nc.dram_tensor(f"routed{c}", (MAX_BLOCKS * P, ROW), F32).ap() for c in range(2)]
        acc = [[nc.dram_tensor(f"acc{c}{a}", (TOKENS + P, DIM), F32).ap() for a in range(2)]
               for c in range(2)]

        x_res = sb("x_res", [P, NT, DIM])
        ident = sb("ident", [P, P])
        before = sb("before", [P, P], BF16)
        ones = sb("ones", [P, P], BF16)
        iota_e = sb("iota_e", [P, NE])
        slot0 = sb("slot0", [P, NE])
        ones_e = sb("ones_e", [P, NE])
        steps_blk = sb("steps_blk", [P, 7])
        steps_grp = sb("steps_grp", [P, 12])
        iota_p = sb("iota_p", [P, 1])
        iota_i = sb("iota_i", [P, P], I32)
        empty_row = sb("empty_row", [P, ROW])
        zeros = sb("zeros", [P, DIM])
        stage = sb("stage", [P, 2 * P])
        gate_w = sb("gate_w", [P, KD, NE])
        wq = sb("wq", [P, KD, QD])
        wk = sb("wk", [P, KD, KVD])
        wv = sb("wv", [P, KD, KVD])
        wo = sb("wo", [P, QC, DIM])
        wq_rows = wo
        wk_rows = wv[:, :, :].rearrange("p k (a n) -> p (k a) n", n=DIM)
        gram = sb("gram", [P, KD, 2, DIM])
        qn = sb("qn", [P, QC])
        kn = sb("kn", [P, KC])
        dist = sb("dist", [P, 2 * P])

        ARENA = 30400
        arena = sb("arena", [P, ARENA])
        used = [0]

        def take(*shape):
            n = 1
            for s in shape:
                n *= s
            v = arena[:, used[0]:used[0] + n]
            used[0] += n
            assert used[0] <= ARENA, used[0]
            names = [f"d{i}" for i in range(len(shape))]
            return v.rearrange(f"p ({' '.join(names)}) -> p {' '.join(names)}",
                               **dict(zip(names, shape))) if len(shape) > 1 else v

        rows = take(NT, TOPK, ROW)
        rows_u = rows.bitcast(U32)
        xT = take(KD, TOKENS)
        w_gu = take(RING, KD, 2 * FFN)
        w_dn = take(RING, 2, DIM)
        blk = take(RING, ROW)
        meta = take(RING, 2)
        blkT = take(2, KD, P)
        silu = take(2, FFN)
        hid = take(2, FFN)
        hidT = take(2, 2, P)
        y_sb = take(RING, DIM)
        onehot = take(NT * TOPK, NE)
        shared_y = onehot.rearrange("p a b -> p (a b)")[:, 0:NT * DIM].rearrange(
            "p (t n) -> p t n", n=DIM)
        probs = take(NT, NE)
        slotm = take(NT, NE)
        pos2 = take(NT, NE)
        sel_used = take(NT * NE // 2)
        sel = sel_used.bitcast(BF16).rearrange("p (t e) -> p t e", e=NE)
        top_v = take(NT, 8)
        top_i = take(NT, 8)
        top_f = take(NT, TOPK)
        slot_f = take(NT * TOPK)
        slot_u = take(NT * TOPK)
        stats = take(NT, 6)
        mv = take(NT, 2)
        rstd = take(NT)
        rmax = take(NT)
        rsum = take(NT)
        rrec = take(NT)
        wsum = take(NT)
        wrec = take(NT)
        more = take(NE, 7)
        extra = take(NE)
        extra_in = take(NE)
        base = take(NE)
        owner = take(1)
        owner_cmp = take(NE)
        grp_cmp = take(12)
        grp_f = take(1)
        table = take(MAX_BLOCKS)
        groups = take(1)
        acc_b = rows.rearrange("p a b c -> p (a b c)")[:, 0:NT * DIM].rearrange(
            "p (t n) -> p t n", n=DIM)

        used[0] = 0
        nbias = take(HEADS, 2 * P)
        proj0 = used[0]
        xn = take(TB, DIM)
        xq = take(TB, DIM)
        xk = take(TB, DIM)
        xnT = take(KD, TB * P)
        xqT = take(KD, TB * P)
        xkT = take(KD, TB * P)
        qT = take(QC, TB * P)
        kT = take(KC, TB * P)
        vx = take(TB, KVH, HD + 1)
        scores = take(2, 2, 2 * P)
        prob = take(2, 2, 2 * P)
        probT = take(2, 2, 2, P)
        heads_o = arena[:, proj0:proj0 + 2 * QD].rearrange("p (b n) -> p b n", b=2)
        headsT = arena[:, proj0 + 2 * QD:proj0 + 3 * QD].rearrange("p (c n) -> p c n", n=P)
        low = take(2, 2)
        osum = take(REP)
        a_stats = take(NT, 6)
        a_mv = take(NT, 2)
        a_rstd = take(NT)
        a_ss = take(TB, 2)
        a_r = take(TB, 2)

        s_x = sem("s_x")
        s_const = sem("s_const")
        s_fix = sem("s_fix")
        s_load = sem("s_load")
        s_attw = sem("s_attw")
        s_rows_w = sem("s_rows_w")
        s_late = sem("s_late")
        s_gram_mm = sem("s_gram_mm")
        s_gram = sem("s_gram")
        s_out = sem("s_out")

        class Moe:
            def __init__(m, c):
                def s(n):
                    return sem(f"m{c}_{n}")
                m.c = c
                m.chain = s("chain")
                m.var = s("var")
                m.std = s("std")
                m.norm = s("norm")
                m.copies = s("copies")
                m.tr = s("tr")
                m.tr_sb = s("tr_sb")
                m.logits = s("logits")
                m.shifted = s("shifted")
                m.expd = s("expd")
                m.sel = s("sel")
                m.rank = s("rank")
                m.owner = s("owner")
                m.ownerT = s("ownerT")
                m.table = s("table")
                m.slots = s("slots")
                m.scat = s("scat")
                m.wsh = s("wsh")
                m.w_gu = [s(f"w_gu{r}") for r in range(RING)]
                m.w_dn = [s(f"w_dn{r}") for r in range(RING)]
                m.blk = [s(f"blk{r}") for r in range(RING)]
                m.meta = s("meta")
                m.gu = s("gu")
                m.silu = s("silu")
                m.hid = s("hid")
                m.hT = s("hT")
                m.hT_sb = s("hT_sb")
                m.down = s("down")
                m.y = s("y")
                m.seed = s("seed")
                m.add = [s(f"add{a}") for a in range(2)]
                m.done = s("done")
                m.sum_ld = s("sum_ld")
                m.x = s("x")
                m.empty = s("empty")

        moe = [Moe(0), Moe(1)]
        a = {n: sem(f"a_{n}") for n in (
            "chain", "norm", "tr", "tr_sb", "u", "scaled", "pj", "pj_act", "pj_dve", "s", "low",
            "p", "pt", "pt_act", "pt_dve", "pv", "on", "ot", "ot_sb", "y", "res", "ones", "bias", "var", "std",
            "ss")}

        block = ctx.enter_context(nc.Block())
        TR, GU, HT, Y = bank[0:2], bank[2:4], bank[4:6], bank[6:8]
        LOGITS, RANK, COUNT = bank[6], bank[7], bank[6]

        N_CONST = 1

        def moe_sync(sp, m):
            c = m.c
            for r in range(2):
                sp.dma_start(w_gu[:, r], sgu_in[r]).then_inc(m.wsh, 16)
                sp.dma_start(w_dn[0:FC, r], sdn_in[r]).then_inc(m.wsh, 16)
            if c == 0:
                sp.dma_start(wq_rows[:, :, :], wqn_in).then_inc(s_rows_w, 16)
                sp.dma_start(wk_rows, wkn_in).then_inc(s_rows_w, 16)
                sp.dma_start(wq[:, :, :], wq_in).then_inc(s_attw, 16)
                sp.dma_start(wk[:, :, :], wk_in).then_inc(s_attw, 16)
            sp.dma_start(acc[c][1][0:TOKENS, :].rearrange("(t p) n -> p t n", p=P),
                         zeros[:, :].unsqueeze(1).broadcast_to([P, NT, DIM])).then_inc(m.seed, 16)
            for k in range(2):
                sp.dma_start(acc[c][k][TOKENS:TOKENS + P, :], zeros[:, :]).then_inc(m.seed, 16)
            sp.wait_ge(m.y, NT)
            sp.dma_start(acc[c][0][0:TOKENS, :].rearrange("(t p) n -> p t n", p=P),
                         shared_y).then_inc(m.seed, 16)
            sp.wait_ge(m.table, 2)
            later = sp.value_load(groups[0:1, 0:1].bitcast(I32), min_val=NE // RING - 1,
                                 max_val=MAX_BLOCKS // RING - 1)
            sp.wait_ge(m.scat, 16 * NT * TOPK)

            def load(s, r, first):
                expert = sp.value_load(table[0:1, bass.ds(s, 1)].bitcast(I32), min_val=0,
                                       max_val=NE - 1)
                if first:
                    if r < 2:
                        sp.wait_ge(m.gu, NSH)
                        sp.wait_ge(m.down, NSH)
                else:
                    sp.wait_ge(m.gu, s + (NSH - RING + 1))
                sp.dma_start(w_gu[:, r], wgu_in[bass.ds(expert, 1)].rearrange(
                    "o p k n -> (o p) k n")).then_inc(m.w_gu[r], 16)
                if not first:
                    sp.wait_ge(m.meta, s - RING + 1)
                sp.dma_start(blk[:, r], routed[c][bass.ds(s * P, P), :]).then_inc(m.blk[r], 16)
                if not first:
                    sp.wait_ge(m.down, s + (NSH - RING + 1))
                sp.dma_start(w_dn[0:FC, r], wdn_in[bass.ds(expert, 1)].rearrange(
                    "o p k n -> (o p) k n")).then_inc(m.w_dn[r], 16)

            for r in range(RING):
                load(r, r, True)
            with sp.Fori(1, later + 1) as grp:
                for r in range(RING):
                    load(grp * RING + r, r, False)
            if c == 0:
                sp.wait_ge(s_gram, 2)
                sp.dma_start(wv[:, :, :], wv_in).then_inc(s_late, 16)
                sp.dma_start(wo[:, :, :], wo_in).then_inc(s_late, 16)
            sp.wait_ge(m.done, 1)
            sp.dma_start(x_res[:, :, :], acc[c][0][0:TOKENS, :].rearrange(
                "(t p) n -> p t n", p=P)).then_inc(m.sum_ld, 16)
            sp.dma_start(acc_b, acc[c][1][0:TOKENS, :].rearrange(
                "(t p) n -> p t n", p=P)).then_inc(m.sum_ld, 16)

        @block.sync
        def _(sp):
            sp.dma_start(x_res[:, :, :], x_in.rearrange("(t p) n -> p t n", p=P)).then_inc(s_x, 16)
            sp.dma_start(gate_w[:, :, :], gate_in).then_inc(s_load, 16)
            sp.dma_start(qn[:, :], qn_in).then_inc(s_load, 16)
            sp.dma_start(kn[:, :], kn_in).then_inc(s_load, 16)
            sp.wait_ge(s_const, N_CONST)
            sp.dma_start(routed[0].rearrange("(b p) n -> p b n", p=P),
                         empty_row[:, :].unsqueeze(1).broadcast_to([P, MAX_BLOCKS, ROW])
                         ).then_inc(moe[0].empty, 16)
            moe_sync(sp, moe[0])
            sp.dma_start(routed[1].rearrange("(b p) n -> p b n", p=P),
                         empty_row[:, :].unsqueeze(1).broadcast_to([P, MAX_BLOCKS, ROW])
                         ).then_inc(moe[1].empty, 16)
            sp.wait_ge(a["res"], NT)
            moe_sync(sp, moe[1])
            sp.wait_ge(moe[1].x, 1)
            sp.dma_start(out.rearrange("(t p) n -> p t n", p=P), x_res[:, :, :]).then_inc(s_out, 16)
            sp.wait_ge(s_out, 16)

        def moe_gpsimd(g, m):
            c = m.c
            if c == 1:
                g.wait_ge(a["res"], NT)
            g.iota(iota_i[:, 0:NT], pattern=[[P, NT]], base=0, channel_multiplier=1
                   ).then_inc(m.copies, 1)
            g.wait_ge(m.copies, 1)
            for t in range(NT):
                g.wait_ge(m.norm, t + 1)
                g.tensor_copy(rows[:, t, 1:TOPK, 0:DIM],
                              rows[:, t, 0, 0:DIM].unsqueeze(1).broadcast_to([P, TOPK - 1, DIM])
                              ).then_inc(m.copies, 1)
            g.tensor_copy(rows_u[:, :, :, DIM + 1],
                          iota_i[:, 0:NT].bitcast(U32).unsqueeze(2).broadcast_to([P, NT, TOPK])
                          ).then_inc(m.copies, 1)
            g.wait_ge(m.copies, NT + 2)
            g.wait_ge(m.empty, 16)
            g.wait_ge(m.slots, 1)
            for t in range(NT):
                for k in range(TOPK):
                    i = t * TOPK + k
                    g.indirect_dma_start(
                        out=routed[c],
                        out_offset=bass.IndirectOffsetOnAxis(
                            ap=slot_u[:, i:i + 1].bitcast(U32), axis=0),
                        in_=rows[:, t, k, :], in_offset=None).then_inc(m.scat, 16)
            g.wait_ge(m.table, 2)
            later = g.value_load(groups[0:1, 0:1].bitcast(I32), min_val=NE // RING - 1,
                                 max_val=MAX_BLOCKS // RING - 1)

            def copy_bits(dst, src):
                return g.tensor_tensor(dst.bitcast(U32), src.bitcast(U32),
                                       zeros[:, 0:2].bitcast(U32), ALU.add)

            def take_meta(r):
                copy_bits(meta[:, r], blk[:, r, DIM:ROW]).then_inc(m.meta, 1)

            def add_rows(r):
                g.indirect_dma_start(
                    out=acc[c][r % 2],
                    out_offset=bass.IndirectOffsetOnAxis(ap=meta[:, r, 1:2].bitcast(U32), axis=0),
                    in_=y_sb[:, r], in_offset=None, compute_op=ALU.add).then_inc(m.add[r % 2], 16)

            for r in range(RING):
                g.wait_ge(m.blk[r], 16)
                if r >= 2:
                    g.wait_ge(m.seed, 64)
                    g.wait_ge(m.y, r + NT - 1)
                take_meta(r)
                if r >= 2:
                    add_rows(r - 2)
            with g.Fori(1, later + 1) as grp:
                for r in range(RING):
                    g.wait_ge(m.add[r % 2], grp * 32 + (16 * (r // 2) - 16))
                    g.wait_ge(m.blk[r], grp * 16 + 16)
                    g.wait_ge(m.y, grp * RING + (r + NT - 1))
                    take_meta(r)
                    add_rows((r - 2) % RING)
            for r in range(2):
                g.wait_ge(m.add[r], later * 32 + 16)
                g.wait_ge(m.y, later * RING + (r + NT + RING - 1))
                copy_bits(stage[:, 8 + 4 * c + 2 * r:10 + 4 * c + 2 * r], zeros[:, 0:2])
                add_rows(r + 2)
            for k in range(2):
                g.wait_ge(m.add[k], later * 32 + 32)
            copy_bits(stage[:, 4 + 2 * c:6 + 2 * c], zeros[:, 0:2]).then_inc(m.done, 1)

        @block.gpsimd
        def _(g):
            n = [0]

            def fix(ins):
                n[0] += 1
                ins.then_inc(s_fix, 1)
                g.wait_ge(s_fix, n[0])

            fix(g.memset(ident[:, :], 0.0))
            fix(g.affine_select(out=ident[:, :], in_=ident[:, :], compare_op=ALU.not_equal,
                                fill=1.0, base=0, pattern=[[-1, P]], channel_multiplier=1))
            fix(g.memset(ones[:, :], 1.0))
            fix(g.affine_select(out=before[:, :], in_=ones[:, :], compare_op=ALU.is_gt,
                                fill=0.0, base=0, pattern=[[1, P]], channel_multiplier=-1))
            fix(g.iota(iota_i[:, 0:NE], pattern=[[1, NE]], base=0, channel_multiplier=0))
            fix(g.tensor_copy(iota_e[:, :], iota_i[:, 0:NE]))
            fix(g.iota(iota_i[:, 0:NE], pattern=[[P, NE]], base=0, channel_multiplier=0))
            fix(g.tensor_copy(slot0[:, :], iota_i[:, 0:NE]))
            fix(g.iota(iota_i[:, 0:7], pattern=[[P, 7]], base=P, channel_multiplier=0))
            fix(g.tensor_copy(steps_blk[:, :], iota_i[:, 0:7]))
            fix(g.iota(iota_i[:, 0:12], pattern=[[RING, 12]], base=0, channel_multiplier=0))
            fix(g.tensor_copy(steps_grp[:, :], iota_i[:, 0:12]))
            fix(g.iota(iota_i[:, 0:1], pattern=[[1, 1]], base=0, channel_multiplier=1))
            fix(g.tensor_copy(iota_p[:, :], iota_i[:, 0:1]))
            fix(g.memset(ones_e[:, :], 1.0))
            fix(g.memset(zeros[:, :], 0.0))
            fix(g.memset(empty_row[:, :], 0.0))
            fix(g.iota(iota_i[:, 0:1], pattern=[[1, 1]], base=TOKENS, channel_multiplier=1))
            fix(g.tensor_copy(empty_row[:, DIM + 1:ROW].bitcast(I32), iota_i[:, 0:1]))
            g.memset(iota_i[:, 0:1], 0).then_inc(s_const, 1)
            dist_i = stage[:, :].bitcast(I32)
            fix(g.iota(dist_i, pattern=[[-1, 2 * P]], base=P, channel_multiplier=1))
            fix(g.tensor_copy(dist[:, :], dist_i))
            fix(g.affine_select(out=dist[:, :], in_=dist[:, :], compare_op=ALU.is_ge, fill=MASKED,
                                base=P, pattern=[[-1, 2 * P]], channel_multiplier=1))
            fix(g.affine_select(out=dist[:, :], in_=dist[:, :], compare_op=ALU.is_ge, fill=MASKED,
                                base=WINDOW - P, pattern=[[1, 2 * P]], channel_multiplier=-1))
            moe_gpsimd(g, moe[0])
            g.wait_ge(moe[0].x, 1)
            ratio = 2.0 ** (-8.0 / HEADS)
            for h in range(HEADS):
                ins = g.tensor_scalar(nbias[:, h, :], dist[:, :], float(ratio ** h), None,
                                      ALU.mult)
            ins.then_inc(a["bias"], 1)
            moe_gpsimd(g, moe[1])

        def moe_tensor(pe, m):
            for t in range(NT):
                pe.wait_ge(m.norm, t + 1)
                if t >= 2:
                    pe.wait_ge(m.tr_sb, t - 1)
                for k in range(KD):
                    mm = pe.transpose(TR[t % 2][:, k * P:(k + 1) * P],
                                      rows[:, t, 0, k * P:(k + 1) * P], ident[:, :])
                mm.then_inc(m.tr, 1)
            for t in range(NT):
                pe.wait_ge(m.tr_sb, t + 1)
                for k in range(KD):
                    mm = pe.matmul(LOGITS[:, t * NE:(t + 1) * NE], xT[:, k, t * P:(t + 1) * P],
                                   gate_w[:, k, :], start=(k == 0), stop=(k == KD - 1))
            mm.then_inc(m.logits, 1)
            pe.wait_ge(m.sel, 1)
            for t in range(NT):
                for j in range(t + 1):
                    pe.matmul(RANK[:, t * NE:(t + 1) * NE],
                              (before if j == t else ones)[:, :], sel[:, j, :],
                              start=(j == 0), stop=(j == t))
            for j in range(NT):
                mm = pe.matmul(COUNT[:, 0:NE], ones[:, :], sel[:, j, :],
                               start=(j == 0), stop=(j == NT - 1))
            mm.then_inc(m.rank, 1)
            pe.wait_ge(m.owner, 1)
            pe.transpose(COUNT[0:1, 128:256], owner[:, 0:1], ident[:, :]).then_inc(m.ownerT, 1)

            def gate_up(q, r, lhs, ring):
                for k in range(KD):
                    mm = pe.matmul(GU[r % 2][:, 0:2 * FFN], lhs(k), w_gu[:, ring, k, :],
                                   start=(k == 0), stop=(k == KD - 1))
                mm.then_inc(m.gu, 1)

            def turn_hidden(q, r, first):
                pe.wait_ge(m.hid, q + 1)
                if not first:
                    pe.wait_ge(m.hT_sb, q - 1)
                for k in range(2):
                    mm = pe.transpose(HT[r % 2][0:FC, k * P:(k + 1) * P],
                                      hid[:, r % 2, k * FC:(k + 1) * FC], ident[:, :])
                mm.then_inc(m.hT, 1)

            def down(q, r, ybank, ring, start, stop):
                pe.wait_ge(m.hT_sb, q + 1)
                for k in range(2):
                    mm = pe.matmul(ybank[:, 0:DIM], hidT[0:FC, r % 2, k, :],
                                   w_dn[0:FC, ring, k, :],
                                   start=(start and k == 0), stop=(stop and k == 1))
                mm.then_inc(m.down, 1)

            pe.wait_ge(m.wsh, 64)
            pe.wait_ge(m.table, 2)
            for q in range(NSH + 2):
                if q >= 2:
                    d = q - 2
                    if d % 2 == 0 and d >= 4:
                        pe.wait_ge(m.y, d // 2 - 1)
                    down(d, d, Y[d // 2 % 2], d % 2, d % 2 == 0, d % 2 == 1)
                if 1 <= q <= NSH:
                    turn_hidden(q - 1, q - 1, q - 1 < 2)
                if q < NSH:
                    if q >= 2:
                        pe.wait_ge(m.hid, q - 1)
                    t = q // 2
                    gate_up(q, q, lambda k: xT[:, k, t * P:(t + 1) * P], q % 2)

            if m.c == 0:
                pe.wait_ge(s_rows_w, 32)
                pe.wait_ge(m.hT_sb, NSH)
                for i, (w, n) in enumerate(((wq_rows, QC), (wk_rows, KC))):
                    for k in range(KD):
                        for j in range(n):
                            mm = pe.matmul(HT[i][:, k * DIM:(k + 1) * DIM],
                                           w[:, j, k * P:(k + 1) * P], w[:, j, :],
                                           start=(j == 0), stop=(j == n - 1))
                    mm.then_inc(s_gram_mm, 1)
                pe.wait_ge(s_gram, 2)

            later = pe.value_load(groups[0:1, 0:1].bitcast(I32), min_val=NE // RING - 1,
                                 max_val=MAX_BLOCKS // RING - 1)

            def step(s, r, first, grp=None):
                group = 0 if first else grp * 16
                pe.wait_ge(m.blk[r], group + 16)
                pe.wait_ge(m.tr_sb, s + (NT - 1))
                for k in range(KD):
                    mm = pe.transpose(TR[r % 2][:, k * P:(k + 1) * P],
                                      blk[:, r, k * P:(k + 1) * P], ident[:, :])
                mm.then_inc(m.tr, 1)
                if not first or r >= 2:
                    rr = (r - 2) % RING
                    pe.wait_ge(m.w_dn[rr], group + (16 if r >= 2 else 0))
                    pe.wait_ge(m.y, s + (NT - 3))
                    down(s + (NSH - 2), rr, Y[rr % 2], rr, True, True)
                if not first or r >= 1:
                    turn_hidden(s + (NSH - 1), (r - 1) % RING, False)
                pe.wait_ge(m.w_gu[r], group + 16)
                pe.wait_ge(m.tr_sb, s + (NT + 1))
                pe.wait_ge(m.hid, s + (NSH - 1))
                gate_up(None, r, lambda k: blkT[:, r % 2, k, :], r)

            for r in range(RING):
                step(r, r, True)
            with pe.Fori(1, later + 1) as grp:
                for r in range(RING):
                    step(grp * RING + r, r, False, grp)
            last = later * RING + RING
            for d in (2, 1):
                pe.wait_ge(m.w_dn[RING - d], later * 16 + 16)
                pe.wait_ge(m.y, last + (NT - d - 1))
                if d == 1:
                    turn_hidden(last + (NSH - 1), RING - 1, False)
                down(last + (NSH - d), RING - d, Y[(RING - d) % 2], RING - d, True, True)

        def attention_tensor(pe):
            X, U, PJ, SC, PT, O = bank[6:8], bank[4:6], bank[0:2], bank[0:2], bank[2:4], bank[4:6]
            pe.wait_ge(s_attw, 32)
            pe.wait_ge(s_load, 48)
            pe.wait_ge(s_late, 32)
            for b in range(BATCHES):
                def turn(i, src, t):
                    if i >= 2:
                        pe.wait_ge(a["tr_sb"], 12 * b + i - 1)
                    for k in range(KD):
                        mm = pe.transpose(X[i % 2][:, k * P:(k + 1) * P],
                                          src[:, t, k * P:(k + 1) * P], ident[:, :])
                    mm.then_inc(a["tr"], 1)

                for t in range(TB):
                    pe.wait_ge(a["norm"], TB * b + t + 1)
                    turn(t, xn, t)
                for t in range(TB):
                    pe.wait_ge(a["tr_sb"], 12 * b + t + 1)
                    if t >= 2:
                        pe.wait_ge(a["ss"], TB * b + t - 1)
                    for k in range(KD):
                        mm = pe.matmul(U[t % 2][:, :], xnT[:, k, t * P:(t + 1) * P],
                                       gram[:, k, :, :].rearrange("p a n -> p (a n)"),
                                       start=(k == 0), stop=(k == KD - 1))
                    mm.then_inc(a["u"], 1)

                def project(i):
                    if i >= 2:
                        pe.wait_ge(a["pj_act" if i % 2 == 0 else "pj_dve"], 12 * b + i // 2)
                    for k in range(KD):
                        if i < TB:
                            l, r = xnT[:, k, i * P:(i + 1) * P], wv[:, k, :]
                        elif i < TB + KC:
                            l, r = wk[:, k, (i - TB) * P:(i - TB + 1) * P], xkT[:, k, :]
                        else:
                            c = i - TB - KC
                            l, r = wq[:, k, c * P:(c + 1) * P], xqT[:, k, :]
                        mm = pe.matmul(PJ[i % 2][:, :], l, r, start=(k == 0), stop=(k == KD - 1))
                    mm.then_inc(a["pj"], 1)

                for i in range(TB):
                    project(i)
                for t in range(TB):
                    pe.wait_ge(a["scaled"], 2 * (TB * b + t + 1))
                    turn(TB + 2 * t, xq, t)
                    turn(TB + 2 * t + 1, xk, t)
                pe.wait_ge(a["tr_sb"], 12 * (b + 1))
                for i in range(TB, TB + KC + QC):
                    project(i)
                pe.wait_ge(a["pj_act"], 12 * (b + 1))
                pe.wait_ge(a["pj_dve"], 12 * (b + 1))

                N = PAIRS * b

                def score(n):
                    t, g, pr = n // 16, n // 2 % KVH, n % 2
                    lo = HD * (g % 2)
                    if n >= 2:
                        pe.wait_ge(a["low"], 2 * (N + n - 1))
                    c0 = 0 if t else P
                    for hh in range(2):
                        c = g // 2 * REP + 2 * pr + hh
                        mm = pe.matmul(SC[n % 2][:, hh * 2 * P + c0:(hh + 1) * 2 * P],
                                       qT[lo:lo + HD, c, t * P:(t + 1) * P],
                                       kT[lo:lo + HD, g // 2, (t - 1) * P + c0:(t + 1) * P],
                                       start=True, stop=True)
                    mm.then_inc(a["s"], 1)

                def turn_probs(n):
                    t = n // 16
                    pe.wait_ge(a["p"], N + n + 1)
                    if n >= 2:
                        pe.wait_ge(a["pt_act" if n % 2 == 0 else "pt_dve"], (N + n) // 2)
                    for hh in range(2):
                        for kt in range(0 if t else 1, 2):
                            mm = pe.transpose(PT[n % 2][:, (2 * hh + kt) * P:(2 * hh + kt + 1) * P],
                                              prob[:, n % 2, hh, kt * P:(kt + 1) * P], ident[:, :])
                    mm.then_inc(a["pt"], 1)

                def values(n):
                    t, g, pr = n // 16, n // 2 % KVH, n % 2
                    u = n // 2
                    pe.wait_ge(a["pt_act" if n % 2 == 0 else "pt_dve"], (N + n) // 2 + 1)
                    if pr == 0 and u >= 2:
                        pe.wait_ge(a["on"], N // 2 + u - 1)
                    for hh in range(2):
                        r = 2 * pr + hh
                        for kt in range(0 if t else 1, 2):
                            mm = pe.matmul(O[u % 2][:, r * (HD + 1):(r + 1) * (HD + 1)],
                                           probT[:, n % 2, hh, kt, :], vx[:, t - 1 + kt, g, :],
                                           start=(kt == (0 if t else 1)), stop=(kt == 1))
                    mm.then_inc(a["pv"], 1)

                def project_out(t):
                    pe.wait_ge(a["on"], N // 2 + KVH * (t + 1))
                    for i in range(4):
                        n = 4 * t + i
                        if i < 2 and t > 0:
                            pe.wait_ge(a["res"], TB * b + t)
                        if i >= 2:
                            pe.wait_ge(a["ot_sb"], 16 * b + n - 1)
                        for j in range(4):
                            mm = pe.transpose(X[i % 2][:, j * P:(j + 1) * P],
                                              heads_o[:, t % 2, (4 * i + j) * P:(4 * i + j + 1) * P],
                                              ident[:, :])
                        mm.then_inc(a["ot"], 1)
                    pe.wait_ge(a["ot_sb"], 16 * b + 4 * (t + 1))
                    for j in range(QC):
                        mm = pe.matmul(X[0][:, 0:DIM], headsT[:, j, :], wo[:, j, :],
                                       start=(j == 0), stop=(j == QC - 1))
                    mm.then_inc(a["y"], 1)

                score(0)
                for n in range(PAIRS + 1):
                    if n + 1 < PAIRS:
                        score(n + 1)
                    if n < PAIRS:
                        turn_probs(n)
                    if n >= 1:
                        values(n - 1)
                    if n % 16 == 2 and n > 16:
                        project_out(n // 16 - 1)
                project_out(TB - 1)
                pe.wait_ge(a["res"], TB * (b + 1))

        @block.tensor
        def _(pe):
            pe.wait_ge(s_const, N_CONST)
            pe.wait_ge(s_load, 48)
            moe_tensor(pe, moe[0])
            attention_tensor(pe)
            moe_tensor(pe, moe[1])

        def moe_scalar(act, m):
            act.wait_ge(m.var, 1)
            nc.scalar.activation(rstd[:, :], rstd[:, :], ACT.Sqrt).then_inc(m.std, 1)
            for t in range(NT):
                act.wait_ge(m.tr, t + 1)
                nc.scalar.copy(xT[:, :, t * P:(t + 1) * P],
                               TR[t % 2][:, 0:DIM].rearrange("p (k n) -> p k n", k=KD)
                               ).then_inc(m.tr_sb, 1)
            act.wait_ge(m.shifted, 1)
            nc.scalar.activation(probs[:, :, :], probs[:, :, :], ACT.Exp).then_inc(m.expd, 1)

            def gated(q, r, first):
                act.wait_ge(m.gu, q + 1)
                if not first:
                    act.wait_ge(m.hid, q - 1)
                nc.scalar.activation(silu[:, r % 2, :], GU[r % 2][:, 0:FFN], ACT.Silu
                                     ).then_inc(m.silu, 1)

            for q in range(NSH):
                gated(q, q, q < 2)
            if m.c == 0:
                for i in range(2):
                    act.wait_ge(s_gram_mm, i + 1)
                    nc.scalar.copy(gram[:, :, i, :],
                                   HT[i][:, :].rearrange("p (k n) -> p k n", k=KD)
                                   ).then_inc(s_gram, 1)
            act.wait_ge(m.table, 2)
            later = act.value_load(groups[0:1, 0:1].bitcast(I32), min_val=NE // RING - 1,
                                 max_val=MAX_BLOCKS // RING - 1)

            def step(s, r, first):
                act.wait_ge(m.tr, s + (NT + 1))
                if not first or r >= 2:
                    act.wait_ge(m.gu, s + (NSH - 1))
                nc.scalar.copy(blkT[:, r % 2], TR[r % 2][:, 0:DIM].rearrange(
                    "p (k n) -> p k n", k=KD)).then_inc(m.tr_sb, 1)
                gated(s + NSH, r, False)

            for r in range(RING):
                step(r, r, True)
            with act.Fori(1, later + 1) as grp:
                for r in range(RING):
                    step(grp * RING + r, r, False)

        def attention_scalar(act):
            X, PJ, PT = bank[6:8], bank[0:2], bank[2:4]
            act.wait_ge(s_load, 48)
            act.wait_ge(a["var"], 1)
            nc.scalar.activation(a_rstd[:, :], a_rstd[:, :], ACT.Sqrt).then_inc(a["std"], 1)
            for b in range(BATCHES):
                for i in range(12):
                    if i == TB:
                        act.wait_ge(a["var"], b + 2)
                        nc.scalar.activation(a_r[:, :, :], a_r[:, :, :], ACT.Sqrt
                                             ).then_inc(a["std"], 1)
                    act.wait_ge(a["tr"], 12 * b + i + 1)
                    if i < TB:
                        dst, t = xnT, i
                    else:
                        dst, t = (xqT, xkT)[(i - TB) % 2], (i - TB) // 2
                    nc.scalar.copy(dst[:, :, t * P:(t + 1) * P],
                                   X[i % 2][:, 0:DIM].rearrange("p (k n) -> p k n", k=KD)
                                   ).then_inc(a["tr_sb"], 1)
                    if i == TB - 1:
                        for j in range(0, TB, 2):
                            act.wait_ge(a["pj"], 24 * b + j + 1)
                            nc.scalar.copy(vx[:, j, :, 0:HD], PJ[0][:, :].rearrange(
                                "p (g d) -> p g d", g=KVH)).then_inc(a["pj_act"], 1)
                for i in range(TB, TB + KC + QC, 2):
                    act.wait_ge(a["pj"], 24 * b + i + 1)
                    if i < TB + KC:
                        dst, w = kT[:, i - TB, :], kn[:, i - TB:i - TB + 1]
                    else:
                        c = i - TB - KC
                        dst, w = qT[:, c, :], qn[:, c:c + 1]
                    nc.scalar.activation(dst, PJ[0][:, :], ACT.Copy, scale=w
                                         ).then_inc(a["pj_act"], 1)
                N = PAIRS * b

                def exps(n):
                    c0 = 0 if n // 16 else P
                    if n >= 2:
                        act.wait_ge(a["pt"], N + n - 1)
                    for hh in range(2):
                        act.wait_ge(a["low"], 2 * (N + n) + hh + 1)
                        e = nc.scalar.activation(prob[:, n % 2, hh, c0:2 * P],
                                                 scores[:, n % 2, hh, c0:2 * P], ACT.Exp,
                                                 bias=low[:, n % 2, hh:hh + 1], scale=-1.0)
                    e.then_inc(a["p"], 1)

                exps(0)
                for n in range(PAIRS + 1):
                    if n + 1 < PAIRS:
                        exps(n + 1)
                    if n < PAIRS and n % 2 == 0:
                        act.wait_ge(a["pt"], N + n + 1)
                        if n >= 2:
                            act.wait_ge(a["pv"], N + n - 1)
                        k0 = 0 if n // 16 else 1
                        nc.scalar.copy(probT[:, 0, :, k0:2, :], PT[0][:, :].rearrange(
                            "p (h k q) -> p h k q", h=2, k=2)[:, :, k0:2, :]
                            ).then_inc(a["pt_act"], 1)
                    if (n % 16 == 2 and n > 16) or n == PAIRS:
                        t = n // 16 - 1
                        for i in range(4):
                            act.wait_ge(a["ot"], 16 * b + 4 * t + i + 1)
                            nc.scalar.copy(headsT[:, 4 * i:4 * i + 4, :], X[i % 2][:, :].rearrange(
                                "p (c n) -> p c n", c=4)).then_inc(a["ot_sb"], 1)

        @block.scalar
        def _(act):
            moe_scalar(act, moe[0])
            act.wait_ge(moe[0].x, 1)
            attention_scalar(act)
            moe_scalar(act, moe[1])

        def layer_norm_stats(v, link, var, std, stats, mv, rstd):
            for t in range(NT):
                ins = v.bn_stats(stats[:, t, :], x_res[:, t, :])
            link(ins)
            for t in range(NT):
                ins = v.bn_aggr(mv[:, t, :], stats[:, t, :])
            link(ins)
            v.tensor_scalar(rstd[:, :], mv[:, :, 1], LN_EPS, None, ALU.add).then_inc(var, 1)
            v.wait_ge(std, 1)
            link(v.reciprocal(rstd[:, :], rstd[:, :]))

        def moe_vector(v, m):
            n = [0]

            def link(ins):
                n[0] += 1
                ins.then_inc(m.chain, 1)
                v.wait_ge(m.chain, n[0])

            if m.c == 0:
                v.wait_ge(s_x, 16)
            layer_norm_stats(v, link, m.var, m.std, stats, mv, rstd)
            for t in range(NT):
                v.tensor_scalar(rows[:, t, 0, 0:DIM], x_res[:, t, :], mv[:, t, 0:1],
                                rstd[:, t:t + 1], ALU.subtract, ALU.mult).then_inc(m.norm, 1)
            v.wait_ge(m.logits, 1)
            logits = LOGITS[:, :].rearrange("p (t e) -> p t e", e=NE)
            link(v.tensor_reduce(rmax[:, :], logits, AX.X, ALU.max))
            v.tensor_tensor(probs[:, :, :], logits, rmax.unsqueeze(2).broadcast_to([P, NT, NE]),
                            ALU.subtract).then_inc(m.shifted, 1)
            v.wait_ge(m.expd, 1)
            link(v.tensor_reduce(rsum[:, :], probs[:, :, :], AX.X, ALU.add))
            link(v.reciprocal(rrec[:, :], rsum[:, :]))
            link(v.tensor_tensor(probs[:, :, :], probs[:, :, :],
                                 rrec.unsqueeze(2).broadcast_to([P, NT, NE]), ALU.mult))
            for t in range(NT):
                link(v.max(top_v[:, t, :], probs[:, t, :]))
                link(v.max_index(top_i[:, t, :].bitcast(U32), top_v[:, t, :], probs[:, t, :]))
            link(v.tensor_copy(top_f[:, :, :], top_i[:, :, 0:TOPK].bitcast(U32)))
            v.wait_ge(s_const, N_CONST)
            link(v.tensor_tensor(onehot[:, :, :],
                                 iota_e[:, :].unsqueeze(1).broadcast_to([P, NT * TOPK, NE]),
                                 top_f.rearrange("p t k -> p (t k)").unsqueeze(2).broadcast_to(
                                     [P, NT * TOPK, NE]), ALU.is_equal))
            with nc.allow_low_precision(reason="sums of at most one 1"):
                v.tensor_reduce(sel, onehot.rearrange("p (t k) e -> p t e k", k=TOPK), AX.X,
                                ALU.add).then_inc(m.sel, 1)
            link(v.tensor_reduce(wsum[:, :], top_v[:, :, 0:TOPK], AX.X, ALU.add))
            link(v.tensor_scalar(wsum[:, :], wsum[:, :], TOPK_EPS, None, ALU.add))
            link(v.reciprocal(wrec[:, :], wsum[:, :]))
            link(v.scalar_tensor_tensor(out=rows[:, :, :, DIM], in0=top_v[:, :, 0:TOPK], scalar=0.5,
                                        in1=wrec.unsqueeze(2).broadcast_to([P, NT, TOPK]),
                                        op0=ALU.mult, op1=ALU.mult))
            v.wait_ge(m.rank, 1)
            link(v.tensor_tensor(more[:, :, :],
                                 COUNT[:, 0:NE].unsqueeze(2).broadcast_to([P, NE, 7]),
                                 steps_blk[:, :].unsqueeze(1).broadcast_to([P, NE, 7]),
                                 ALU.is_gt))
            link(v.tensor_reduce(extra[:, :], more[:, :, :], AX.X, ALU.add))
            link(v.tensor_tensor_scan(extra_in[:, :], ones_e[:, :], extra[:, :], 0.0, ALU.mult,
                                      ALU.add))
            link(v.tensor_tensor(base[:, :], extra_in[:, :], extra[:, :], ALU.subtract))
            link(v.tensor_scalar(base[:, :], base[:, :], float(P), float((NE - 1) * P), ALU.mult,
                                 ALU.add))
            link(v.tensor_tensor(base[:, :], base[:, :], slot0[:, :], ALU.subtract))
            rank = RANK[:, :].rearrange("p (t e) -> p t e", e=NE)
            link(v.scalar_tensor_tensor(out=pos2[:, :, :], in0=rank, scalar=float(P),
                                        in1=base.unsqueeze(1).broadcast_to([P, NT, NE]),
                                        op0=ALU.is_ge, op1=ALU.mult))
            link(v.tensor_tensor(slotm[:, :, :], rank,
                                 slot0[:, :].unsqueeze(1).broadcast_to([P, NT, NE]), ALU.add))
            link(v.tensor_tensor(slotm[:, :, :], slotm[:, :, :], pos2[:, :, :], ALU.add))
            link(v.tensor_tensor(onehot.rearrange("p (t k) e -> p t k e", k=TOPK),
                                 onehot.rearrange("p (t k) e -> p t k e", k=TOPK),
                                 slotm.unsqueeze(2).broadcast_to([P, NT, TOPK, NE]), ALU.mult))
            link(v.tensor_reduce(slot_f[:, :], onehot[:, :, :], AX.X, ALU.add))
            v.tensor_copy(slot_u.bitcast(U32), slot_f[:, :]).then_inc(m.slots, 1)
            link(v.tensor_scalar(owner_cmp[:, :], extra_in[:, :], iota_p[:, 0:1], 0.0, ALU.is_le,
                                 ALU.add, accum_out=owner[:, 0:1]))
            v.tensor_scalar(owner[:, 0:1], owner[:, 0:1], float(NE - 1), None, ALU.min
                            ).then_inc(m.owner, 1)
            v.wait_ge(m.ownerT, 1)
            link(v.tensor_copy(table[0:1, NE:MAX_BLOCKS].bitcast(I32),
                               COUNT[0:1, 128:128 + MAX_EXTRA]))
            v.tensor_copy(table[0:1, 0:NE].bitcast(I32), iota_e[0:1, :]).then_inc(m.table, 1)
            link(v.tensor_scalar(grp_cmp[0:1, :], steps_grp[0:1, :],
                                 extra_in[0:1, NE - 1:NE], float(NE // RING - 1), ALU.is_lt, ALU.add,
                                 accum_out=grp_f[0:1, :]))
            v.tensor_copy(groups[0:1, :].bitcast(I32), grp_f[0:1, :]).then_inc(m.table, 1)

            def hidden(q, r, first):
                v.wait_ge(m.silu, q + 1)
                if not first:
                    v.wait_ge(m.hT, q - 1)
                v.tensor_tensor(hid[:, r % 2, :], silu[:, r % 2, :], GU[r % 2][:, FFN:2 * FFN],
                                ALU.mult).then_inc(m.hid, 1)

            def hidden_T(q, r, first):
                v.wait_ge(m.hT, q + 1)
                if not first:
                    v.wait_ge(m.down, q - 1)
                v.tensor_copy(hidT[0:FC, r % 2], HT[r % 2][0:FC, 0:2 * P].rearrange(
                    "p (k n) -> p k n", k=2)).then_inc(m.hT_sb, 1)

            for q in range(NSH + 2):
                if q >= 2 and q % 2 == 1:
                    t = (q - 2) // 2
                    v.wait_ge(m.down, 2 * t + 2)
                    if t == 0:
                        v.wait_ge(m.slots, 1)
                    v.scalar_tensor_tensor(out=shared_y[:, t, :], in0=Y[t % 2][:, 0:DIM],
                                           scalar=0.5, in1=x_res[:, t, :], op0=ALU.mult,
                                           op1=ALU.add).then_inc(m.y, 1)
                if 1 <= q <= NSH:
                    hidden_T(q - 1, q - 1, q - 1 < 2)
                if q < NSH:
                    hidden(q, q, q < 2)
            later = v.value_load(groups[0:1, 0:1].bitcast(I32), min_val=NE // RING - 1,
                                 max_val=MAX_BLOCKS // RING - 1)

            def weighted(s, r):
                v.wait_ge(m.down, s + (NSH + 1))
                v.wait_ge(m.meta, s + 1)
                v.tensor_scalar(y_sb[:, r], Y[r % 2][:, 0:DIM], meta[:, r, 0:1], None, ALU.mult
                                ).then_inc(m.y, 1)

            def step(s, r, first):
                if not first or r >= 2:
                    weighted(s - 2, (r - 2) % RING)
                if not first or r >= 1:
                    hidden_T(s + (NSH - 1), (r - 1) % RING, False)
                hidden(s + NSH, r, False)

            for r in range(RING):
                step(r, r, True)
            with v.Fori(1, later + 1) as grp:
                for r in range(RING):
                    step(grp * RING + r, r, False)
            last = later * RING + RING
            weighted(last - 2, RING - 2)
            hidden_T(last + (NSH - 1), RING - 1, False)
            weighted(last - 1, RING - 1)
            v.wait_ge(m.sum_ld, 32)
            v.tensor_tensor(x_res[:, :, :], x_res[:, :, :], acc_b, ALU.add).then_inc(m.x, 1)
            v.wait_ge(m.x, 1)

        def attention_vector(v):
            U, PJ, SC, PT, O, X = bank[4:6], bank[0:2], bank[0:2], bank[2:4], bank[4:6], bank[6:8]
            v.memset(vx[:, :, :, HD:HD + 1], 1.0).then_inc(a["ones"], 1)
            n_chain = [0]

            def link(ins):
                n_chain[0] += 1
                ins.then_inc(a["chain"], 1)
                v.wait_ge(a["chain"], n_chain[0])

            v.wait_ge(s_load, 48)
            layer_norm_stats(v, link, a["var"], a["std"], a_stats, a_mv, a_rstd)
            for b in range(BATCHES):
                for t in range(TB):
                    tt = b * TB + t
                    v.tensor_scalar(xn[:, t, :], x_res[:, tt, :], a_mv[:, tt, 0:1],
                                    a_rstd[:, tt:tt + 1],
                                    ALU.subtract, ALU.mult).then_inc(a["norm"], 1)
                for t in range(TB):
                    v.wait_ge(a["u"], TB * b + t + 1)
                    v.wait_ge(a["norm"], TB * b + t + 1)
                    for i, width in enumerate((QD, KVD)):
                        ins = v.tensor_tensor_reduce((xq, xk)[i][:, t, :], xn[:, t, :],
                                                     U[t % 2][:, i * DIM:(i + 1) * DIM],
                                                     1.0 / width, 0.0, ALU.mult, ALU.add,
                                                     a_ss[:, t, i:i + 1])
                    ins.then_inc(a["ss"], 1)
                v.wait_ge(a["ss"], TB * (b + 1))
                v.tensor_scalar(a_r[:, :, :], a_ss[:, :, :], RMS_EPS, None, ALU.add
                                ).then_inc(a["var"], 1)
                v.wait_ge(a["std"], b + 2)
                link(v.reciprocal(a_r[:, :, :], a_r[:, :, :]))
                for t in range(TB):
                    v.tensor_scalar(xq[:, t, :], xn[:, t, :], a_r[:, t, 0:1],
                                    -float(HD) ** -0.5, ALU.mult, ALU.mult
                                    ).then_inc(a["scaled"], 1)
                    v.tensor_scalar(xk[:, t, :], xn[:, t, :], a_r[:, t, 1:2], None, ALU.mult
                                    ).then_inc(a["scaled"], 1)
                for i in range(1, TB + KC + QC, 2):
                    v.wait_ge(a["pj"], 24 * b + i + 1)
                    if i < TB:
                        v.tensor_copy(vx[:, i, :, 0:HD], PJ[1][:, :].rearrange(
                            "p (g d) -> p g d", g=KVH)).then_inc(a["pj_dve"], 1)
                        continue
                    if i < TB + KC:
                        dst, w = kT[:, i - TB, :], kn[:, i - TB:i - TB + 1]
                    else:
                        c = i - TB - KC
                        dst, w = qT[:, c, :], qn[:, c:c + 1]
                    v.tensor_scalar(dst, PJ[1][:, :], w, None, ALU.mult).then_inc(a["pj_dve"], 1)
                N = PAIRS * b

                def biased(n):
                    t, g, pr = n // 16, n // 2 % KVH, n % 2
                    c0 = 0 if t else P
                    v.wait_ge(a["s"], N + n + 1)
                    if n >= 2:
                        v.wait_ge(a["p"], N + n - 1)
                    for hh in range(2):
                        h = REP * g + 2 * pr + hh
                        v.tensor_tensor_reduce(scores[:, n % 2, hh, c0:2 * P],
                                               nbias[:, h, c0:2 * P],
                                               SC[n % 2][:, hh * 2 * P + c0:(hh + 1) * 2 * P],
                                               1.0, 3e38, ALU.add, ALU.min,
                                               low[:, n % 2, hh:hh + 1]).then_inc(a["low"], 1)

                v.wait_ge(a["bias"], 1)
                biased(0)
                for n in range(PAIRS + 1):
                    if n + 1 < PAIRS:
                        biased(n + 1)
                    if n % 2 == 1:
                        v.wait_ge(a["pt"], N + n + 1)
                        if n >= 2:
                            v.wait_ge(a["pv"], N + n - 1)
                        k0 = 0 if n // 16 else 1
                        v.tensor_copy(probT[:, 1, :, k0:2, :], PT[1][:, :].rearrange(
                            "p (h k q) -> p h k q", h=2, k=2)[:, :, k0:2, :]
                            ).then_inc(a["pt_dve"], 1)
                    if n >= 2 and n % 2 == 0:
                        u = n // 2 - 1
                        t, g = u // KVH, u % KVH
                        v.wait_ge(a["pv"], N + n)
                        if g == 0 and t >= 2:
                            v.wait_ge(a["ot"], 16 * b + 4 * (t - 1))
                        o = O[u % 2][:, 0:REP * (HD + 1)].rearrange("p (r d) -> p r d", r=REP)
                        link(v.reciprocal(osum[:, :], o[:, :, HD]))
                        v.tensor_tensor(heads_o[:, t % 2, g * REP * HD:(g + 1) * REP * HD]
                                        .rearrange("p (r d) -> p r d", r=REP), o[:, :, 0:HD],
                                        osum.unsqueeze(2).broadcast_to([P, REP, HD]), ALU.mult
                                        ).then_inc(a["on"], 1)
                    if (n % 16 == 2 and n > 16) or n == PAIRS:
                        t = n // 16 - 1
                        v.wait_ge(a["y"], TB * b + t + 1)
                        v.tensor_tensor(x_res[:, b * TB + t, :], X[0][:, 0:DIM],
                                        x_res[:, b * TB + t, :], ALU.add).then_inc(a["res"], 1)
            v.wait_ge(a["res"], NT)

        @block.vector
        def _(v):
            moe_vector(v, moe[0])
            attention_vector(v)
            moe_vector(v, moe[1])


def kernel(**inputs):
    import numpy as np
    import concourse.bacc as bacc
    from concourse.bass_utils import run_bass_kernel_spmd as run

    def f(n):
        return np.asarray(inputs[n])

    c = np.ascontiguousarray

    def by_rows(w):
        return c(w.reshape(w.shape[0] // P, P, w.shape[1]).transpose(1, 0, 2))

    wq, wk, wv, wo = (f("L0_attn_" + n) for n in ("wq", "wk", "wv", "wo"))
    order = [REP * (2 * j + half) + r for j in range(KVH // 2) for r in range(REP)
             for half in range(2)]
    wqp = wq.reshape(HEADS, HD, DIM)[order].reshape(QD, DIM)
    qnp = f("L0_attn_q_norm_w").reshape(HEADS, HD)[order].reshape(QC, P)
    gu = f("L0_ffn_w_gate_up")
    dn = f("L0_ffn_w_down")
    sgu = f("L0_ffn_ws_gate_up").reshape(2, 2, FFN, DIM).transpose(1, 0, 2, 3).reshape(
        2, 2 * FFN, DIM)
    sdn = f("L0_ffn_ws_down")
    arrays = {
        "x": c(f("L0_attn_x").reshape(TOKENS, DIM)),
        "gate": by_rows(f("L0_ffn_gate_w").T),
        "wgu": c(gu.transpose(0, 2, 1).reshape(NE, KD, P, 2 * FFN).transpose(0, 2, 1, 3)),
        "wdn": c(dn.transpose(0, 2, 1).reshape(NE, 2, FC, DIM).transpose(0, 2, 1, 3)),
        "sgu": c(sgu.transpose(0, 2, 1).reshape(2, KD, P, 2 * FFN).transpose(0, 2, 1, 3)),
        "sdn": c(sdn.T.reshape(2, 2, FC, DIM).transpose(0, 2, 1, 3)),
        "wq": by_rows(wqp.T),
        "wqn": by_rows(wq),
        "wk": by_rows(wk.T),
        "wkn": by_rows(wk),
        "wv": by_rows(wv.T),
        "wo": by_rows(wo.T),
        "qn": c(qnp.T),
        "kn": c(f("L0_attn_k_norm_w").reshape(KC, P).T),
    }
    nc = bacc.Bacc("TRN2", target_bir_lowering=False, num_devices=1)
    args = [nc.dram_tensor(f"in_{n}", v.shape, mybir.dt.from_np(v.dtype),
                           kind="ExternalInput").ap() for n, v in arrays.items()]
    args.append(nc.dram_tensor("out", (TOKENS, DIM), F32, kind="ExternalOutput").ap())
    macaron(nc, *args)
    r = run(nc, [{f"in_{n}": v for n, v in arrays.items()}], core_ids=[0])
    return r.results[0]["out"].reshape(inputs["L0_attn_x"].shape)
```

```python
from contextlib import ExitStack

import concourse.bass as bass
from concourse import mybir

F32 = mybir.dt.float32
BF16 = mybir.dt.bfloat16
F16 = mybir.dt.float16
I32 = mybir.dt.int32
U32 = mybir.dt.uint32
ALU = mybir.AluOpType
ACT = mybir.ActivationFunctionType
AX = mybir.AxisListType

P = 128
DIM = 256
KD = DIM // P
TOKENS = 1024
NT = TOKENS // P
BATCHES = 2
TB = NT // BATCHES
CHUNK = 2
NE = 64
TOPK = 6
FFN = 176
FC = FFN // 2
RING = 4
ROW = DIM + NE
MAX_EXTRA = 48
MAX_BLOCKS = NE + MAX_EXTRA
NSH = 2 * NT
HEADS = 32
KVH = 8
HD = 64
REP = HEADS // KVH
QD = HEADS * HD
KVD = KVH * HD
QC = QD // P
KC = KVD // P
WINDOW = 128
MASKED = 1e34
ALIBI_RATIO = 2.0 ** (-8.0 / HEADS)
PAIRS = TB * KVH * 2
LN_EPS, RMS_EPS, TOPK_EPS = 1e-5, 1e-6, 1e-20


def macaron(nc, x_in, gate_in, wgu_in, wdn_in, sgu_in, sdn_in, wq_in, wqn_in, wk_in, wkn_in,
            wv_in, wo_in, qn_in, kn_in, out):
    ctx = ExitStack()
    with ctx:
        def sb(name, shape, dt=F32):
            return ctx.enter_context(nc.sbuf_tensor(name, shape, dt))

        def sem(name):
            return ctx.enter_context(nc.semaphore(name))

        bank = [ctx.enter_context(nc.psum_tensor(f"bank{i}", [P, 512], F32)) for i in range(8)]

        table_x = [nc.dram_tensor(f"table_x{c}", (P + TOKENS, ROW), F32).ap() for c in range(2)]
        acc = [[nc.dram_tensor(f"acc{c}{a}", (P + TOKENS, DIM), F32).ap() for a in range(2)]
               for c in range(2)]

        x_res = sb("x_res", [P, NT, DIM])
        ident = sb("ident", [P, P])
        before = sb("before", [P, P], BF16)
        ones = sb("ones", [P, P], BF16)
        iota_e = sb("iota_e", [P, NE])
        slot0 = sb("slot0", [P, NE])
        ones_e = sb("ones_e", [P, NE])
        steps_blk = sb("steps_blk", [P, 7])
        steps_grp = sb("steps_grp", [P, 12])
        iota_p = sb("iota_p", [P, 1])
        iota_i = sb("iota_i", [P, P], I32)
        iota_r = sb("iota_r", [P, P])
        row_id = sb("row_id", [P, NT])
        zeros = sb("zeros", [P, ROW])
        stage = sb("stage", [P, 2 * P])
        gate_w = sb("gate_w", [P, KD, NE])
        wq = sb("wq", [P, KD, QD])
        wk = sb("wk", [P, KD, KVD])
        wv = sb("wv", [P, KD, KVD])
        wo = sb("wo", [P, QC, DIM])
        wq_rows = wo
        wk_rows = wv[:, :, :].rearrange("p k (a n) -> p (k a) n", n=DIM)
        gram = sb("gram", [P, KD, 2, DIM])
        qn = sb("qn", [P, QC])
        kn = sb("kn", [P, KC])
        dist = sb("dist", [P, 2 * P])

        ARENA = 33472
        arena = sb("arena", [P, ARENA])
        used = [0]

        def take(*shape):
            n = 1
            for s in shape:
                n *= s
            v = arena[:, used[0]:used[0] + n]
            used[0] += n
            assert used[0] <= ARENA, used[0]
            names = [f"d{i}" for i in range(len(shape))]
            return v.rearrange(f"p ({' '.join(names)}) -> p {' '.join(names)}",
                               **dict(zip(names, shape))) if len(shape) > 1 else v

        rows = take(NT, ROW)
        xT = take(KD, TOKENS)
        w_gu = take(RING, KD, 2 * FFN)
        w_dn = take(RING, 2, DIM)
        ws_gu = take(2, KD, 2 * FFN)
        ws_dn = take(2, 2, DIM)
        blkT = take(2, KD, P)
        silu = take(2, FFN)
        up = take(2, FFN)
        hid = take(2, FFN)
        hidT = take(2, 2, P)
        meta = take(RING)
        gidx = take(RING)
        aidx = take(RING)
        shared_y = take(NT, DIM)
        onehot = take(NT * TOPK * NE // 2).bitcast(BF16).rearrange("p (c e) -> p c e", e=NE)
        pair_sum = take(NT * 3 * NE // 2).bitcast(BF16).rearrange("p (t k e) -> p t k e", k=3, e=NE)
        routing0 = used[0]
        at_slot = take(NT * TOPK * P // 2).bitcast(F16).rearrange("p (c r) -> p c r", r=P)
        at_block = take(NT * TOPK * MAX_BLOCKS // 2).bitcast(F16).rearrange(
            "p (c n) -> p c n", n=MAX_BLOCKS)
        routing1 = used[0]
        used[0] = routing0
        onehot_slot = take(NT * TOPK, NE)
        used[0] = routing0
        blk = take(RING, ROW)
        y_sb = take(RING, DIM)
        used[0] = routing0
        acc_b = take(NT, DIM)
        used[0] = routing1
        probs = take(NT, NE)
        slotm = take(NT, NE)
        pos2 = take(NT, NE)
        sel_used = take(NT * NE // 2)
        sel = sel_used.bitcast(BF16).rearrange("p (t e) -> p t e", e=NE)
        top_v = take(NT, 8)
        top_i = take(NT, 8)
        top_f = take(NT, TOPK)
        slot_f = take(NT * TOPK)
        slot_u = take(NT * TOPK)
        place_u = take(2, NT * TOPK)
        place_f = take(2, NT * TOPK)
        slot_row = take(MAX_BLOCKS + RING)
        factor = take(NT)
        stats = take(NT, 6)
        mv = take(NT, 2)
        rstd = take(NT)
        rmax = take(NT)
        rsum = take(NT)
        rrec = take(NT)
        wsum = take(NT)
        wrec = take(NT)
        more = take(NE, 7)
        extra = take(NE)
        extra_in = take(NE)
        base = take(NE)
        owner = take(1)
        owner_cmp = take(NE)
        grp_cmp = take(12)
        grp_f = take(1)
        table = take(MAX_BLOCKS)
        groups = take(1)
        used[0] = 0
        nbias = take(HEADS, 2 * P)
        proj0 = used[0]
        xn = take(TB, DIM)
        xq = take(TB, DIM)
        xk = take(TB, DIM)
        xnT = take(KD, TB * P)
        xqT = take(KD, TB * P)
        xkT = take(KD, TB * P)
        qT = take(QC, 2, TB * P // 2).bitcast(F16)
        kT = take(KVH, 2, TB * P // 2).bitcast(F16)
        q_low = take(4, TB * P // 2).bitcast(F16)
        vx = take(TB, KVH, HD + 1)
        scores = take(2, 2, 2 * P)
        prob = take(2, 2, 2 * P)
        probT = take(2, 2, 2, P)
        heads_o = arena[:, proj0:proj0 + 2 * QD].rearrange("p (b n) -> p b n", b=2)
        headsT = arena[:, proj0 + 2 * QD:proj0 + 3 * QD].rearrange("p (c n) -> p c n", n=P)
        low = take(2, 2)
        osum = take(REP)
        a_stats = take(NT, 6)
        a_mv = take(NT, 2)
        a_rstd = take(NT)
        a_ss = take(TB, 2)
        a_r = take(TB, 2)

        s_x = sem("s_x")
        s_const = sem("s_const")
        s_fix = sem("s_fix")
        s_load = sem("s_load")
        s_attw = sem("s_attw")
        s_rows_w = sem("s_rows_w")
        s_late = sem("s_late")
        s_gram_mm = sem("s_gram_mm")
        s_gram = sem("s_gram")
        s_out = sem("s_out")

        class Moe:
            def __init__(m, c):
                def s(n):
                    return sem(f"m{c}_{n}")
                m.c = c
                m.chain = s("chain")
                m.var = s("var")
                m.std = s("std")
                m.norm = s("norm")
                m.tr = s("tr")
                m.tr_sb = s("tr_sb")
                m.logits = s("logits")
                m.shifted = s("shifted")
                m.expd = s("expd")
                m.sel = s("sel")
                m.rank = s("rank")
                m.onehots = s("onehots")
                m.scaled = s("scaled")
                m.ids = s("ids")
                m.asked = s("asked")
                m.gid = s("gid")
                m.owner = s("owner")
                m.ownerT = s("ownerT")
                m.table = s("table")
                m.comb = s("comb")
                m.tab = s("tab")
                m.wsh = s("wsh")
                m.w_gu = [s(f"w_gu{r}") for r in range(RING)]
                m.w_dn = [s(f"w_dn{r}") for r in range(RING)]
                m.blk = [s(f"blk{r}") for r in range(RING)]
                m.gu = s("gu")
                m.silu = s("silu")
                m.hid = s("hid")
                m.half = s("half")
                m.hT = s("hT")
                m.hT_sb = s("hT_sb")
                m.down = s("down")
                m.ysh = s("ysh")
                m.y = s("y")
                m.seed = s("seed")
                m.add = [s(f"add{a}") for a in range(2)]
                m.done = s("done")
                m.sum_ld = [s(f"sum_ld{i}") for i in range(NT // CHUNK)]
                m.x = s("x")

        moe = [Moe(0), Moe(1)]
        a = {n: sem(f"a_{n}") for n in (
            "chain", "norm", "tr", "tr_sb", "u", "scaled", "pj", "pj_act", "pj_dve", "hi", "lo", "s", "low",
            "p", "pt", "pt_act", "pt_dve", "pv", "on", "ot", "ot_sb", "y", "res", "ones", "bias", "var", "std",
            "ss")}

        a_moved = [sem(f"a_moved{i}") for i in range(4)]

        block = ctx.enter_context(nc.Block())
        TR, GU, HT, Y = bank[0:2], bank[2:4], bank[4:6], bank[6:8]
        LOGITS, RANK, COUNT, IDS, OWNER = bank[6], bank[1], bank[0], bank[1], bank[0]
        IDS0, OWNER0 = 0, P

        N_CONST = 1
        RANKS_AT = 4

        def moe_sync(sp, m):
            c = m.c
            for r in range(2):
                sp.dma_start(ws_gu[:, r], sgu_in[r]).then_inc(m.wsh, 16)
                sp.dma_start(ws_dn[0:FC, r], sdn_in[r]).then_inc(m.wsh, 16)
            for r in range(RING):
                sp.dma_start(w_gu[:, r], wgu_in[r]).then_inc(m.w_gu[r], 16)
                sp.dma_start(w_dn[0:FC, r], wdn_in[r]).then_inc(m.w_dn[r], 16)
            if c == 0:
                sp.dma_start(wq_rows[:, :, :], wqn_in).then_inc(s_rows_w, 16)
                sp.dma_start(wk_rows, wkn_in).then_inc(s_rows_w, 16)
                sp.dma_start(wq[:, :, :], wq_in).then_inc(s_attw, 16)
                sp.dma_start(wk[:, :, :], wk_in).then_inc(s_attw, 16)
            sp.dma_start(table_x[c][0:P, :], zeros[:, :]).then_inc(m.tab, 16)
            sp.dma_start(acc[c][1][P:, :].rearrange("(t p) n -> p t n", p=P),
                         zeros[:, 0:DIM].unsqueeze(1).broadcast_to([P, NT, DIM])
                         ).then_inc(m.seed, 16)
            for k in range(2):
                sp.dma_start(acc[c][k][0:P, :], zeros[:, 0:DIM]).then_inc(m.seed, 16)
            sp.wait_ge(m.comb, 1)
            sp.dma_start(table_x[c][P:, :].rearrange("(t p) n -> p t n", p=P), rows
                         ).then_inc(m.tab, 16)
            sp.wait_ge(m.ysh, NT)
            sp.dma_start(acc[c][0][P:, :].rearrange("(t p) n -> p t n", p=P),
                         shared_y).then_inc(m.seed, 16)
            sp.wait_ge(m.table, 2)
            later = sp.value_load(groups[0:1, 0:1].bitcast(I32), min_val=NE // RING - 1,
                                 max_val=MAX_BLOCKS // RING - 1)
            with sp.Fori(1, later + 1) as grp:
                for r in range(RING):
                    s = grp * RING + r
                    expert = sp.value_load(table[0:1, bass.ds(s, 1)].bitcast(I32), min_val=0,
                                           max_val=NE - 1)
                    sp.wait_ge(m.gu, s + (NSH - RING + 1))
                    sp.dma_start(w_gu[:, r], wgu_in[bass.ds(expert, 1)].rearrange(
                        "o p k n -> (o p) k n")).then_inc(m.w_gu[r], 16)
                    sp.wait_ge(m.down, s + (NSH - RING + 1))
                    sp.dma_start(w_dn[0:FC, r], wdn_in[bass.ds(expert, 1)].rearrange(
                        "o p k n -> (o p) k n")).then_inc(m.w_dn[r], 16)
            if c == 0:
                sp.wait_ge(s_gram, 2)
                sp.dma_start(wv[:, :, :], wv_in).then_inc(s_late, 16)
                sp.dma_start(wo[:, :, :], wo_in).then_inc(s_late, 16)
            sp.wait_ge(m.done, 1)
            for t in range(0, NT, CHUNK):
                for k, dst in enumerate((x_res, acc_b)):
                    sp.dma_start(dst[:, t:t + CHUNK, :], acc[c][k][P * (t + 1):P * (t + CHUNK + 1), :]
                                 .rearrange("(t p) n -> p t n", p=P)).then_inc(m.sum_ld[t // CHUNK],
                                                                               16)

        @block.sync
        def _(sp):
            sp.dma_start(x_res[:, :, :], x_in.rearrange("(t p) n -> p t n", p=P)).then_inc(s_x, 16)
            sp.dma_start(gate_w[:, :, :], gate_in).then_inc(s_load, 16)
            sp.dma_start(qn[:, :], qn_in).then_inc(s_load, 16)
            sp.dma_start(kn[:, :], kn_in).then_inc(s_load, 16)
            sp.wait_ge(s_const, N_CONST)
            moe_sync(sp, moe[0])
            for b in range(BATCHES):
                for i in range(KC + QC):
                    sp.wait_ge(a["lo"], (KC + QC) * b + i + 1)
                    for half in range(2):
                        mine = slice(HD * half, HD * (half + 1))
                        other = slice(HD * (1 - half), HD * (2 - half))
                        if i < KC:
                            dst, src = kT[other, 2 * i + half], kT[mine, 2 * i + half]
                        else:
                            dst, src = qT[other, i - KC, half], q_low[mine, i % 4]
                        sp.dma_start(dst, src).then_inc(a_moved[i % 4], 16)
            sp.wait_ge(a["res"], NT)
            moe_sync(sp, moe[1])
            for t in range(0, NT, CHUNK):
                sp.wait_ge(moe[1].x, t // CHUNK + 1)
                sp.dma_start(out[t * P:(t + CHUNK) * P, :].rearrange("(t p) n -> p t n", p=P),
                             x_res[:, t:t + CHUNK, :]).then_inc(s_out, 16)
            sp.wait_ge(s_out, 16 * (NT // CHUNK))

        def moe_gpsimd(g, m):
            c = m.c
            for q in range(NSH + 2):
                if q >= 2 and q % 2 == 1:
                    t = (q - 2) // 2
                    g.wait_ge(m.half, t + 1)
                    g.tensor_tensor(shared_y[:, t, :], shared_y[:, t, :], x_res[:, t, :], ALU.add
                                    ).then_inc(m.ysh, 1)
                if q < NSH:
                    g.wait_ge(m.silu, q + 1)
                    if q >= 2:
                        g.wait_ge(m.hT, q - 1)
                    g.tensor_tensor(hid[:, q % 2, :], silu[:, q % 2, :], up[:, q % 2, :],
                                    ALU.mult).then_inc(m.hid, 1)

            def waited():
                g.sem_inc(m.asked, 1)

            def gather(r):
                g.indirect_dma_start(
                    out=blk[:, r], out_offset=None, in_=table_x[c],
                    in_offset=bass.IndirectOffsetOnAxis(ap=gidx[:, r:r + 1].bitcast(U32), axis=0)
                    ).then_inc(m.blk[r], 16)

            def add_rows(r):
                g.indirect_dma_start(
                    out=acc[c][r % 2],
                    out_offset=bass.IndirectOffsetOnAxis(ap=aidx[:, r:r + 1].bitcast(U32), axis=0),
                    in_=y_sb[:, r], in_offset=None, compute_op=ALU.add).then_inc(m.add[r % 2], 16)

            g.wait_ge(m.tab, 32)
            g.wait_ge(m.gid, RING)
            for r in range(RING):
                gather(r)
            g.wait_ge(m.table, 2)
            later = g.value_load(groups[0:1, 0:1].bitcast(I32), min_val=NE // RING - 1,
                                 max_val=MAX_BLOCKS // RING - 1)
            g.wait_ge(m.seed, 64)

            def serve(grp, r, first):
                g.wait_ge(m.gid, grp * RING + (r + 1))
                if not first:
                    waited()
                gather(r)
                g.wait_ge(m.y, grp * RING + (r - RING + 1))
                if not first:
                    g.wait_ge(m.add[r % 2], grp * 32 + (16 * (r // 2) - 32))
                    waited()
                elif r >= 2:
                    g.wait_ge(m.add[r % 2], 16)
                add_rows(r)

            for r in range(RING):
                serve(1, r, True)
            with g.Fori(2, later + 1) as grp:
                for r in range(RING):
                    serve(grp, r, False)
            for r in range(RING):
                g.wait_ge(m.y, later * RING + (r + 1))
                g.wait_ge(m.add[r % 2], later * 32 + 16 * (r // 2))
                waited()
                add_rows(r)
            for k in range(2):
                g.wait_ge(m.add[k], later * 32 + 32)
            g.tensor_tensor(stage[:, 2 * c:2 * c + 2], zeros[:, 0:2], zeros[:, 0:2], ALU.add
                            ).then_inc(m.done, 1)

        @block.gpsimd
        def _(g):
            n = [0]

            def fix(ins):
                n[0] += 1
                ins.then_inc(s_fix, 1)
                g.wait_ge(s_fix, n[0])

            fix(g.memset(ident[:, :], 0.0))
            fix(g.affine_select(out=ident[:, :], in_=ident[:, :], compare_op=ALU.not_equal,
                                fill=1.0, base=0, pattern=[[-1, P]], channel_multiplier=1))
            fix(g.memset(ones[:, :], 1.0))
            fix(g.affine_select(out=before[:, :], in_=ones[:, :], compare_op=ALU.is_gt,
                                fill=0.0, base=0, pattern=[[1, P]], channel_multiplier=-1))
            fix(g.iota(iota_i[:, 0:NE], pattern=[[1, NE]], base=0, channel_multiplier=0))
            fix(g.tensor_copy(iota_e[:, :], iota_i[:, 0:NE]))
            fix(g.iota(iota_i[:, 0:NE], pattern=[[P, NE]], base=0, channel_multiplier=0))
            fix(g.tensor_copy(slot0[:, :], iota_i[:, 0:NE]))
            fix(g.iota(iota_i[:, 0:7], pattern=[[P, 7]], base=P, channel_multiplier=0))
            fix(g.tensor_copy(steps_blk[:, :], iota_i[:, 0:7]))
            fix(g.iota(iota_i[:, 0:12], pattern=[[RING, 12]], base=0, channel_multiplier=0))
            fix(g.tensor_copy(steps_grp[:, :], iota_i[:, 0:12]))
            fix(g.iota(iota_i[:, 0:1], pattern=[[1, 1]], base=0, channel_multiplier=1))
            fix(g.tensor_copy(iota_p[:, :], iota_i[:, 0:1]))
            fix(g.memset(ones_e[:, :], 1.0))
            fix(g.memset(zeros[:, :], 0.0))
            fix(g.iota(iota_i[:, :], pattern=[[1, P]], base=0, channel_multiplier=0))
            fix(g.tensor_copy(iota_r[:, :], iota_i[:, :]))
            fix(g.iota(iota_i[:, 0:NT], pattern=[[P, NT]], base=P, channel_multiplier=1))
            fix(g.tensor_copy(row_id[:, :], iota_i[:, 0:NT]))
            g.memset(iota_i[:, 0:1], 0).then_inc(s_const, 1)
            dist_i = stage[:, :].bitcast(I32)
            fix(g.iota(dist_i, pattern=[[-1, 2 * P]], base=P, channel_multiplier=1))
            fix(g.tensor_copy(dist[:, :], dist_i))
            fix(g.affine_select(out=dist[:, :], in_=dist[:, :], compare_op=ALU.is_ge, fill=MASKED,
                                base=P, pattern=[[-1, 2 * P]], channel_multiplier=1))
            fix(g.affine_select(out=dist[:, :], in_=dist[:, :], compare_op=ALU.is_ge, fill=MASKED,
                                base=WINDOW - P, pattern=[[1, 2 * P]], channel_multiplier=-1))
            moe_gpsimd(g, moe[0])
            moe_gpsimd(g, moe[1])

        def moe_tensor(pe, m):
            for t in range(NT + 1):
                if t < NT:
                    pe.wait_ge(m.norm, t + 1)
                    if t >= 2:
                        pe.wait_ge(m.tr_sb, t - 1)
                    for k in range(KD):
                        mm = pe.transpose(TR[t % 2][:, k * P:(k + 1) * P],
                                          rows[:, t, k * P:(k + 1) * P], ident[:, :])
                    mm.then_inc(m.tr, 1)
                if t >= 1:
                    pe.wait_ge(m.tr_sb, t)
                    for k in range(KD):
                        mm = pe.matmul(LOGITS[:, (t - 1) * NE:t * NE],
                                       xT[:, k, (t - 1) * P:t * P], gate_w[:, k, :],
                                       start=(k == 0), stop=(k == KD - 1))
            mm.then_inc(m.logits, 1)

            def ranks():
                pe.wait_ge(m.sel, 1)
                for j in range(NT):
                    pe.matmul(COUNT[:, 0:NE], ones[:, :], sel[:, j, :],
                              start=(j == 0), stop=(j == NT - 1))
                for t in range(NT):
                    for j in range(t + 1):
                        mm = pe.matmul(RANK[:, t * NE:(t + 1) * NE],
                                       (before if j == t else ones)[:, :], sel[:, j, :],
                                       start=(j == 0), stop=(j == t))
                mm.then_inc(m.rank, 1)

            def gate_up(r, lhs, weights):
                for k in range(KD):
                    mm = pe.matmul(GU[r % 2][:, 0:2 * FFN], lhs(k), weights[:, k, :],
                                   start=(k == 0), stop=(k == KD - 1))
                mm.then_inc(m.gu, 1)

            def turn_hidden(q, r, first):
                pe.wait_ge(m.hid, q + 1)
                if not first:
                    pe.wait_ge(m.hT_sb, q - 1)
                for k in range(2):
                    mm = pe.transpose(HT[r % 2][0:FC, k * P:(k + 1) * P],
                                      hid[:, r % 2, k * FC:(k + 1) * FC], ident[:, :])
                mm.then_inc(m.hT, 1)

            def down(q, r, ybank, weights, start, stop):
                pe.wait_ge(m.hT_sb, q + 1)
                for k in range(2):
                    mm = pe.matmul(ybank[:, 0:DIM], hidT[0:FC, r % 2, k, :],
                                   weights[0:FC, k, :],
                                   start=(start and k == 0), stop=(stop and k == 1))
                mm.then_inc(m.down, 1)

            pe.wait_ge(m.wsh, 64)
            for q in range(NSH + 2):
                if q == RANKS_AT:
                    ranks()
                if q < NSH:
                    if q >= 2:
                        pe.wait_ge(m.hid, q - 1)
                    t = q // 2
                    gate_up(q, lambda k: xT[:, k, t * P:(t + 1) * P], ws_gu[:, q % 2])
                if q >= 2:
                    d = q - 2
                    if d == 0:
                        pe.wait_ge(m.shifted, 1)
                    if d % 2 == 0 and d >= 4:
                        pe.wait_ge(m.half, d // 2 - 1)
                    down(d, d, Y[d // 2 % 2], ws_dn[:, d % 2], d % 2 == 0, d % 2 == 1)
                if 1 <= q <= NSH:
                    turn_hidden(q - 1, q - 1, q - 1 < 2)

            if m.c == 0:
                pe.wait_ge(s_rows_w, 32)
                pe.wait_ge(m.hT_sb, NSH)
                for i, (w, n) in enumerate(((wq_rows, QC), (wk_rows, KC))):
                    for k in range(KD):
                        for j in range(n):
                            mm = pe.matmul(HT[i][:, k * DIM:(k + 1) * DIM],
                                           w[:, j, k * P:(k + 1) * P], w[:, j, :],
                                           start=(j == 0), stop=(j == n - 1))
                    mm.then_inc(s_gram_mm, 1)

            for i in range(NT * TOPK):
                if i % TOPK == 0:
                    pe.wait_ge(m.scaled, i // TOPK + 1)
                mm = pe.matmul(IDS[:, IDS0:IDS0 + MAX_BLOCKS], at_slot[:, i, :], at_block[:, i, :],
                               start=(i == 0), stop=(i == NT * TOPK - 1))
            mm.then_inc(m.ids, 1)
            pe.wait_ge(m.owner, 1)
            pe.transpose(OWNER[0:1, OWNER0:OWNER0 + P], owner[:, 0:1], ident[:, :]
                         ).then_inc(m.ownerT, 1)
            pe.wait_ge(m.table, 2)
            if m.c == 0:
                pe.wait_ge(s_gram, 2)
            later = pe.value_load(groups[0:1, 0:1].bitcast(I32), min_val=NE // RING - 1,
                                 max_val=MAX_BLOCKS // RING - 1)

            def step(s, r, first, grp=None):
                group = 0 if first else grp * 16
                pe.wait_ge(m.blk[r], group + 16)
                pe.wait_ge(m.tr_sb, s + (NT - 1))
                for k in range(KD):
                    mm = pe.transpose(TR[r % 2][:, k * P:(k + 1) * P],
                                      blk[:, r, k * P:(k + 1) * P], ident[:, :])
                mm.then_inc(m.tr, 1)
                if not first or r >= 2:
                    rr = (r - 2) % RING
                    pe.wait_ge(m.w_dn[rr], group + (16 if r >= 2 else 0))
                    if first:
                        pe.wait_ge(m.half, NT)
                    else:
                        pe.wait_ge(m.y, s - 3)
                    down(s + (NSH - 2), rr, Y[rr % 2], w_dn[:, rr], True, True)
                if not first or r >= 1:
                    turn_hidden(s + (NSH - 1), (r - 1) % RING, False)
                pe.wait_ge(m.w_gu[r], group + 16)
                pe.wait_ge(m.tr_sb, s + (NT + 1))
                pe.wait_ge(m.hid, s + (NSH - 1))
                gate_up(r, lambda k: blkT[:, r % 2, k, :], w_gu[:, r])

            for r in range(RING):
                step(r, r, True)
            with pe.Fori(1, later + 1) as grp:
                for r in range(RING):
                    step(grp * RING + r, r, False, grp)
            last = later * RING + RING
            for d in (2, 1):
                pe.wait_ge(m.w_dn[RING - d], later * 16 + 16)
                pe.wait_ge(m.y, last - (d + 1))
                if d == 1:
                    turn_hidden(last + (NSH - 1), RING - 1, False)
                down(last + (NSH - d), RING - d, Y[(RING - d) % 2], w_dn[:, RING - d], True, True)

        def attention_tensor(pe):
            X, U, PJ, SC, PT, O = bank[6:8], bank[4:6], bank[0:4], bank[0:2], bank[2:4], bank[4:6]
            pe.wait_ge(s_attw, 32)
            pe.wait_ge(s_load, 48)
            pe.wait_ge(s_late, 32)
            for b in range(BATCHES):
                def turn(i, src, t):
                    if i >= 2:
                        pe.wait_ge(a["tr_sb"], 12 * b + i - 1)
                    for k in range(KD):
                        mm = pe.transpose(X[i % 2][:, k * P:(k + 1) * P],
                                          src[:, t, k * P:(k + 1) * P], ident[:, :])
                    mm.then_inc(a["tr"], 1)

                for t in range(TB):
                    pe.wait_ge(a["norm"], TB * b + t + 1)
                    turn(t, xn, t)
                for t in range(TB):
                    pe.wait_ge(a["tr_sb"], 12 * b + t + 1)
                    if t >= 2:
                        pe.wait_ge(a["ss"], TB * b + t - 1)
                    for k in range(KD):
                        mm = pe.matmul(U[t % 2][:, :], xnT[:, k, t * P:(t + 1) * P],
                                       gram[:, k, :, :].rearrange("p a n -> p (a n)"),
                                       start=(k == 0), stop=(k == KD - 1))
                    mm.then_inc(a["u"], 1)

                def project(i):
                    if TB <= i < 2 * TB:
                        pe.wait_ge(a["pj_act" if i % 2 == 0 else "pj_dve"],
                                   2 * b + (i - TB) // 2 + 1)
                    elif i >= 2 * TB:
                        pe.wait_ge(a["lo"], (KC + QC) * b + i - 2 * TB + 1)
                    for k in range(KD):
                        if i < TB:
                            l, r = xnT[:, k, i * P:(i + 1) * P], wv[:, k, :]
                        elif i < TB + KC:
                            l, r = wk[:, k, (i - TB) * P:(i - TB + 1) * P], xkT[:, k, :]
                        else:
                            c = i - TB - KC
                            l, r = wq[:, k, c * P:(c + 1) * P], xqT[:, k, :]
                        mm = pe.matmul(PJ[i % 4][:, :], l, r, start=(k == 0), stop=(k == KD - 1))
                    mm.then_inc(a["pj"], 1)

                for i in range(TB):
                    project(i)
                for t in range(TB):
                    pe.wait_ge(a["scaled"], 2 * (TB * b + t + 1))
                    turn(TB + 2 * t, xq, t)
                    turn(TB + 2 * t + 1, xk, t)
                pe.wait_ge(a["tr_sb"], 12 * (b + 1))
                for i in range(TB, TB + KC + QC):
                    project(i)
                pe.wait_ge(a["lo"], (KC + QC) * (b + 1))
                for i in range(4):
                    pe.wait_ge(a_moved[i], 8 * (KC + QC) * (b + 1))

                N = PAIRS * b

                def score(n):
                    t, g, pr = n // 16, n // 2 % KVH, n % 2
                    if n >= 2:
                        pe.wait_ge(a["low"], 2 * (N + n - 1))
                    c0 = 0 if t else P
                    for hh in range(2):
                        c = g // 2 * REP + 2 * pr + hh
                        for part in range(2):
                            mm = pe.matmul(SC[n % 2][:, hh * 2 * P + c0:(hh + 1) * 2 * P],
                                           qT[:, c, g % 2, t * P:(t + 1) * P],
                                           kT[:, g, part, (t - 1) * P + c0:(t + 1) * P],
                                           start=(part == 0), stop=(part == 1))
                    mm.then_inc(a["s"], 1)

                def turn_probs(n):
                    t = n // 16
                    pe.wait_ge(a["p"], N + n + 1)
                    if n >= 2:
                        pe.wait_ge(a["pt_act" if n % 2 == 0 else "pt_dve"], (N + n) // 2)
                    for hh in range(2):
                        for kt in range(0 if t else 1, 2):
                            mm = pe.transpose(PT[n % 2][:, (2 * hh + kt) * P:(2 * hh + kt + 1) * P],
                                              prob[:, n % 2, hh, kt * P:(kt + 1) * P], ident[:, :])
                    mm.then_inc(a["pt"], 1)

                def values(n):
                    t, g, pr = n // 16, n // 2 % KVH, n % 2
                    u = n // 2
                    pe.wait_ge(a["pt_act" if n % 2 == 0 else "pt_dve"], (N + n) // 2 + 1)
                    if pr == 0 and u >= 2:
                        pe.wait_ge(a["on"], N // 2 + u - 1)
                    for hh in range(2):
                        r = 2 * pr + hh
                        for kt in range(0 if t else 1, 2):
                            mm = pe.matmul(O[u % 2][:, r * (HD + 1):(r + 1) * (HD + 1)],
                                           probT[:, n % 2, hh, kt, :], vx[:, t - 1 + kt, g, :],
                                           start=(kt == (0 if t else 1)), stop=(kt == 1))
                    mm.then_inc(a["pv"], 1)

                def project_out(t):
                    pe.wait_ge(a["on"], N // 2 + KVH * (t + 1))
                    for i in range(4):
                        n = 4 * t + i
                        if i < 2 and t > 0:
                            pe.wait_ge(a["res"], TB * b + t)
                        if i >= 2:
                            pe.wait_ge(a["ot_sb"], 16 * b + n - 1)
                        for j in range(4):
                            mm = pe.transpose(X[i % 2][:, j * P:(j + 1) * P],
                                              heads_o[:, t % 2, (4 * i + j) * P:(4 * i + j + 1) * P],
                                              ident[:, :])
                        mm.then_inc(a["ot"], 1)
                    pe.wait_ge(a["ot_sb"], 16 * b + 4 * (t + 1))
                    for j in range(QC):
                        mm = pe.matmul(X[0][:, 0:DIM], headsT[:, j, :], wo[:, j, :],
                                       start=(j == 0), stop=(j == QC - 1))
                    mm.then_inc(a["y"], 1)

                score(0)
                for n in range(PAIRS + 1):
                    if n + 1 < PAIRS:
                        score(n + 1)
                    if n < PAIRS:
                        turn_probs(n)
                    if n >= 1:
                        values(n - 1)
                    if n % 16 == 2 and n > 16:
                        project_out(n // 16 - 1)
                project_out(TB - 1)
                pe.wait_ge(a["res"], TB * (b + 1))

        @block.tensor
        def _(pe):
            pe.wait_ge(s_const, N_CONST)
            pe.wait_ge(s_load, 48)
            moe_tensor(pe, moe[0])
            attention_tensor(pe)
            moe_tensor(pe, moe[1])

        def moe_scalar(act, m):
            act.wait_ge(m.var, 1)
            nc.scalar.activation(rstd[:, :], rstd[:, :], ACT.Sqrt).then_inc(m.std, 1)
            for t in range(NT):
                act.wait_ge(m.tr, t + 1)
                nc.scalar.copy(xT[:, :, t * P:(t + 1) * P],
                               TR[t % 2][:, 0:DIM].rearrange("p (k n) -> p k n", k=KD)
                               ).then_inc(m.tr_sb, 1)
            act.wait_ge(m.shifted, 1)
            nc.scalar.activation(probs[:, :, :], probs[:, :, :], ACT.Exp).then_inc(m.expd, 1)

            def gated(q, r, first, shared=False):
                act.wait_ge(m.gu, q + 1)
                if not first:
                    act.wait_ge(m.hid, q - 1)
                if shared:
                    nc.scalar.copy(up[:, r % 2, :], GU[r % 2][:, FFN:2 * FFN])
                nc.scalar.activation(silu[:, r % 2, :], GU[r % 2][:, 0:FFN], ACT.Silu
                                     ).then_inc(m.silu, 1)

            for q in range(NSH + 2):
                if q < NSH:
                    gated(q, q, q < 2, True)
                if q >= 2 and q % 2 == 1:
                    t = (q - 2) // 2
                    act.wait_ge(m.down, 2 * t + 2)
                    nc.scalar.mul(shared_y[:, t, :], Y[t % 2][:, 0:DIM], 0.5).then_inc(m.half, 1)
                if not 1 <= q <= NSH:
                    continue
                p = q - 1
                act.wait_ge(m.hT, p + 1)
                if p >= 2:
                    act.wait_ge(m.down, p - 1)
                nc.scalar.copy(hidT[0:FC, p % 2], HT[p % 2][0:FC, 0:2 * P].rearrange(
                    "p (k n) -> p k n", k=2)).then_inc(m.hT_sb, 1)
            if m.c == 0:
                for i in range(2):
                    act.wait_ge(s_gram_mm, i + 1)
                    nc.scalar.copy(gram[:, :, i, :],
                                   HT[i][:, :].rearrange("p (k n) -> p k n", k=KD)
                                   ).then_inc(s_gram, 1)
            for t in range(NT):
                act.wait_ge(m.onehots, t + 1)
                ch = slice(t * TOPK, (t + 1) * TOPK)
                nc.scalar.activation(at_block[:, ch, :], at_block[:, ch, :], ACT.Copy,
                                     scale=row_id[:, t:t + 1]).then_inc(m.scaled, 1)
            act.wait_ge(m.table, 2)
            later = act.value_load(groups[0:1, 0:1].bitcast(I32), min_val=NE // RING - 1,
                                 max_val=MAX_BLOCKS // RING - 1)

            def step(s, r, first):
                act.wait_ge(m.tr, s + (NT + 1))
                if not first or r >= 2:
                    act.wait_ge(m.gu, s + (NSH - 1))
                nc.scalar.copy(blkT[:, r % 2], TR[r % 2][:, 0:DIM].rearrange(
                    "p (k n) -> p k n", k=KD)).then_inc(m.tr_sb, 1)
                gated(s + NSH, r, False)

            for r in range(RING):
                step(r, r, True)
            with act.Fori(1, later + 1) as grp:
                for r in range(RING):
                    step(grp * RING + r, r, False)

        def attention_scalar(act):
            X, PJ, PT = bank[6:8], bank[0:4], bank[2:4]
            act.wait_ge(s_load, 48)
            act.wait_ge(a["var"], 1)
            nc.scalar.activation(a_rstd[:, :], a_rstd[:, :], ACT.Sqrt).then_inc(a["std"], 1)
            for b in range(BATCHES):
                for i in range(12):
                    if i == TB:
                        act.wait_ge(a["var"], b + 2)
                        nc.scalar.activation(a_r[:, :, :], a_r[:, :, :], ACT.Sqrt
                                             ).then_inc(a["std"], 1)
                    act.wait_ge(a["tr"], 12 * b + i + 1)
                    if i < TB:
                        dst, t = xnT, i
                    else:
                        dst, t = (xqT, xkT)[(i - TB) % 2], (i - TB) // 2
                    nc.scalar.copy(dst[:, :, t * P:(t + 1) * P],
                                   X[i % 2][:, 0:DIM].rearrange("p (k n) -> p k n", k=KD)
                                   ).then_inc(a["tr_sb"], 1)
                    if i == TB - 1:
                        for j in range(0, TB, 2):
                            act.wait_ge(a["pj"], 24 * b + j + 1)
                            nc.scalar.copy(vx[:, j, :, 0:HD], PJ[j][:, :].rearrange(
                                "p (g d) -> p g d", g=KVH)).then_inc(a["pj_act"], 1)
                for i in range(KC + QC):
                    act.wait_ge(a["pj"], 24 * b + TB + i + 1)
                    for half in range(2):
                        mine = slice(HD * half, HD * (half + 1))
                        if i < KC:
                            dst, w = kT[mine, 2 * i + half, 0], kn[mine, i:i + 1]
                        else:
                            dst, w = qT[mine, i - KC, half], qn[mine, i - KC:i - KC + 1]
                        ins = nc.scalar.activation(dst, PJ[i % 4][mine, :], ACT.Copy, scale=w)
                    ins.then_inc(a["hi"], 1)
                    if b == 0 and i % 2 == 1:
                        n_now = HEADS * (i + 1) // (KC + QC)
                        for h in range(HEADS * (i - 1) // (KC + QC), n_now):
                            ins = nc.scalar.activation(nbias[:, h, :], dist[:, :], ACT.Copy,
                                                       scale=float(ALIBI_RATIO ** h))
                        if n_now == HEADS:
                            ins.then_inc(a["bias"], 1)
                N = PAIRS * b

                def exps(n):
                    c0 = 0 if n // 16 else P
                    if n >= 2:
                        act.wait_ge(a["pt"], N + n - 1)
                    for hh in range(2):
                        act.wait_ge(a["low"], 2 * (N + n) + hh + 1)
                        e = nc.scalar.activation(prob[:, n % 2, hh, c0:2 * P],
                                                 scores[:, n % 2, hh, c0:2 * P], ACT.Exp,
                                                 bias=low[:, n % 2, hh:hh + 1], scale=-1.0)
                    e.then_inc(a["p"], 1)

                exps(0)
                for n in range(PAIRS + 1):
                    if n + 1 < PAIRS:
                        exps(n + 1)
                    if n < PAIRS and n % 2 == 0:
                        act.wait_ge(a["pt"], N + n + 1)
                        if n >= 2:
                            act.wait_ge(a["pv"], N + n - 1)
                        k0 = 0 if n // 16 else 1
                        nc.scalar.copy(probT[:, 0, :, k0:2, :], PT[0][:, :].rearrange(
                            "p (h k q) -> p h k q", h=2, k=2)[:, :, k0:2, :]
                            ).then_inc(a["pt_act"], 1)
                    if (n % 16 == 2 and n > 16) or n == PAIRS:
                        t = n // 16 - 1
                        for i in range(4):
                            act.wait_ge(a["ot"], 16 * b + 4 * t + i + 1)
                            nc.scalar.copy(headsT[:, 4 * i:4 * i + 4, :], X[i % 2][:, :].rearrange(
                                "p (c n) -> p c n", c=4)).then_inc(a["ot_sb"], 1)

        @block.scalar
        def _(act):
            moe_scalar(act, moe[0])
            act.wait_ge(moe[0].x, NT // CHUNK + 1)
            attention_scalar(act)
            moe_scalar(act, moe[1])

        def token_stats(v, link, stats):
            for t in range(NT):
                ins = v.bn_stats(stats[:, t, :], x_res[:, t, :])
            link(ins)

        def layer_norm_stats(v, link, var, std, stats, mv, rstd):
            for t in range(NT):
                ins = v.bn_aggr(mv[:, t, :], stats[:, t, :])
            link(ins)
            v.tensor_scalar(rstd[:, :], mv[:, :, 1], LN_EPS, None, ALU.add).then_inc(var, 1)
            v.wait_ge(std, 1)
            link(v.reciprocal(rstd[:, :], rstd[:, :]))

        def moe_vector(v, m):
            n = [0]

            def link(ins):
                n[0] += 1
                ins.then_inc(m.chain, 1)
                v.wait_ge(m.chain, n[0])

            if m.c == 0:
                v.wait_ge(s_x, 16)
            token_stats(v, link, stats)
            layer_norm_stats(v, link, m.var, m.std, stats, mv, rstd)
            for t in range(NT):
                v.tensor_scalar(rows[:, t, 0:DIM], x_res[:, t, :], mv[:, t, 0:1],
                                rstd[:, t:t + 1], ALU.subtract, ALU.mult).then_inc(m.norm, 1)
            v.wait_ge(m.logits, 1)
            logits = LOGITS[:, :].rearrange("p (t e) -> p t e", e=NE)
            link(v.tensor_reduce(rmax[:, :], logits, AX.X, ALU.max))
            v.tensor_tensor(probs[:, :, :], logits, rmax.unsqueeze(2).broadcast_to([P, NT, NE]),
                            ALU.subtract).then_inc(m.shifted, 1)
            v.wait_ge(m.expd, 1)
            for t in range(NT):
                ins = v.max(top_v[:, t, :], probs[:, t, :])
            link(ins)
            for t in range(NT):
                ins = v.max_index(top_i[:, t, :].bitcast(U32), top_v[:, t, :], probs[:, t, :])
            link(ins)
            link(v.tensor_copy(top_f[:, :, :], top_i[:, :, 0:TOPK].bitcast(U32)))
            v.wait_ge(s_const, N_CONST)
            link(v.tensor_tensor(onehot[:, :, :],
                                 iota_e[:, :].unsqueeze(1).broadcast_to([P, NT * TOPK, NE]),
                                 top_f.rearrange("p t k -> p (t k)").unsqueeze(2).broadcast_to(
                                     [P, NT * TOPK, NE]), ALU.is_equal))
            by_token = onehot.rearrange("p (t k) e -> p t k e", k=TOPK)
            link(v.tensor_tensor(pair_sum[:, :, :, :], by_token[:, :, 0:3, :],
                                 by_token[:, :, 3:6, :], ALU.add))
            link(v.tensor_tensor(sel, pair_sum[:, :, 0, :], pair_sum[:, :, 1, :], ALU.add))
            v.tensor_tensor(sel, sel, pair_sum[:, :, 2, :], ALU.add).then_inc(m.sel, 1)
            link(v.tensor_reduce(rsum[:, :], probs[:, :, :], AX.X, ALU.add))
            link(v.reciprocal(rrec[:, :], rsum[:, :]))
            link(v.tensor_reduce(wsum[:, :], top_v[:, :, 0:TOPK], AX.X, ALU.add))
            link(v.tensor_tensor(wsum[:, :], wsum[:, :], rrec[:, :], ALU.mult))
            link(v.tensor_scalar(wsum[:, :], wsum[:, :], TOPK_EPS, None, ALU.add))
            link(v.reciprocal(wrec[:, :], wsum[:, :]))
            link(v.tensor_tensor(factor[:, :], wrec[:, :], rrec[:, :], ALU.mult))
            v.wait_ge(m.sel, 1)
            link(v.scalar_tensor_tensor(out=rows[:, :, DIM:ROW], in0=probs[:, :, :], scalar=0.5,
                                        in1=sel, op0=ALU.mult, op1=ALU.mult))
            v.tensor_tensor(rows[:, :, DIM:ROW], rows[:, :, DIM:ROW],
                            factor.unsqueeze(2).broadcast_to([P, NT, NE]), ALU.mult
                            ).then_inc(m.comb, 1)
            v.wait_ge(m.rank, 1)
            link(v.tensor_tensor(more[:, :, :],
                                 COUNT[:, 0:NE].unsqueeze(2).broadcast_to([P, NE, 7]),
                                 steps_blk[:, :].unsqueeze(1).broadcast_to([P, NE, 7]),
                                 ALU.is_gt))
            link(v.tensor_reduce(extra[:, :], more[:, :, :], AX.X, ALU.add))
            link(v.tensor_tensor_scan(extra_in[:, :], ones_e[:, :], extra[:, :], 0.0, ALU.mult,
                                      ALU.add))
            link(v.tensor_tensor(base[:, :], extra_in[:, :], extra[:, :], ALU.subtract))
            link(v.tensor_scalar(base[:, :], base[:, :], float(P), float((NE - 1) * P), ALU.mult,
                                 ALU.add))
            link(v.tensor_tensor(base[:, :], base[:, :], slot0[:, :], ALU.subtract))
            rank = RANK[:, :].rearrange("p (t e) -> p t e", e=NE)
            link(v.scalar_tensor_tensor(out=pos2[:, :, :], in0=rank, scalar=float(P),
                                        in1=base.unsqueeze(1).broadcast_to([P, NT, NE]),
                                        op0=ALU.is_ge, op1=ALU.mult))
            link(v.tensor_tensor(slotm[:, :, :], rank,
                                 slot0[:, :].unsqueeze(1).broadcast_to([P, NT, NE]), ALU.add))
            link(v.tensor_tensor(slotm[:, :, :], slotm[:, :, :], pos2[:, :, :], ALU.add))
            link(v.tensor_tensor(onehot_slot.rearrange("p (t k) e -> p t k e", k=TOPK), by_token,
                                 slotm.unsqueeze(2).broadcast_to([P, NT, TOPK, NE]), ALU.mult))
            link(v.tensor_reduce(slot_f[:, :], onehot_slot[:, :, :], AX.X, ALU.add))
            link(v.tensor_copy(slot_u.bitcast(U32), slot_f[:, :]))
            v.tensor_scalar(place_u[:, 0, :].bitcast(U32), slot_u.bitcast(U32), P - 1, None,
                            ALU.bitwise_and)
            link(v.tensor_scalar(place_u[:, 1, :].bitcast(U32), slot_u.bitcast(U32), 7, None,
                                 ALU.logical_shift_right))
            link(v.tensor_copy(place_f[:, :, :], place_u.bitcast(U32)))
            link(v.tensor_scalar(owner_cmp[:, :], extra_in[:, :], iota_p[:, 0:1], 0.0, ALU.is_le,
                                 ALU.add, accum_out=owner[:, 0:1]))
            v.tensor_scalar(owner[:, 0:1], owner[:, 0:1], float(NE - 1), None, ALU.min
                            ).then_inc(m.owner, 1)
            for t in range(NT):
                ch = slice(t * TOPK, (t + 1) * TOPK)
                v.tensor_tensor(at_slot[:, ch, :],
                                iota_r[:, :].unsqueeze(1).broadcast_to([P, TOPK, P]),
                                place_f[:, 0, ch].unsqueeze(2).broadcast_to([P, TOPK, P]),
                                ALU.is_equal)
                v.tensor_tensor(at_block[:, ch, :],
                                iota_r[:, 0:MAX_BLOCKS].unsqueeze(1).broadcast_to(
                                    [P, TOPK, MAX_BLOCKS]),
                                place_f[:, 1, ch].unsqueeze(2).broadcast_to(
                                    [P, TOPK, MAX_BLOCKS]), ALU.is_equal).then_inc(m.onehots, 1)
            v.memset(slot_row[:, MAX_BLOCKS:], 0.0)
            v.wait_ge(m.ids, 1)
            link(v.tensor_scalar(slot_row[:, 0:MAX_BLOCKS].bitcast(U32),
                                 IDS[:, IDS0:IDS0 + MAX_BLOCKS], iota_p[:, 0:1], None, ALU.max))
            v.tensor_copy(gidx.bitcast(U32), slot_row[:, 0:RING].bitcast(U32)
                          ).then_inc(m.gid, RING)
            v.wait_ge(m.ownerT, 1)
            link(v.tensor_copy(table[0:1, NE:MAX_BLOCKS].bitcast(I32),
                               OWNER[0:1, OWNER0:OWNER0 + MAX_EXTRA]))
            v.tensor_copy(table[0:1, 0:NE].bitcast(I32), iota_e[0:1, :]).then_inc(m.table, 1)
            link(v.tensor_scalar(grp_cmp[0:1, :], steps_grp[0:1, :],
                                 extra_in[0:1, NE - 1:NE], float(NE // RING - 1), ALU.is_lt, ALU.add,
                                 accum_out=grp_f[0:1, :]))
            v.tensor_copy(groups[0:1, :].bitcast(I32), grp_f[0:1, :]).then_inc(m.table, 1)

            def hidden(q, r, first):
                v.wait_ge(m.silu, q + 1)
                if not first:
                    v.wait_ge(m.hT, q - 1)
                v.tensor_tensor(hid[:, r % 2, :], silu[:, r % 2, :], GU[r % 2][:, FFN:2 * FFN],
                                ALU.mult).then_inc(m.hid, 1)

            def hidden_T(q, r, first):
                v.wait_ge(m.hT, q + 1)
                if not first:
                    v.wait_ge(m.down, q - 1)
                v.tensor_copy(hidT[0:FC, r % 2], HT[r % 2][0:FC, 0:2 * P].rearrange(
                    "p (k n) -> p k n", k=2)).then_inc(m.hT_sb, 1)

            v.wait_ge(m.table, 2)
            later = v.value_load(groups[0:1, 0:1].bitcast(I32), min_val=NE // RING - 1,
                                 max_val=MAX_BLOCKS // RING - 1)

            def keep(s, r, first):
                expert = v.value_load(table[0:1, bass.ds(s, 1)].bitcast(I32), min_val=0,
                                      max_val=NE - 1)
                v.wait_ge(m.tr, s + (NT + 1))
                if not first:
                    v.wait_ge(m.y, s - (RING - 1))
                v.tensor_copy(meta[:, r:r + 1], blk[:, r, bass.ds(expert + DIM, 1)])
                v.tensor_copy(gidx[:, r:r + 1].bitcast(U32),
                              slot_row[:, bass.ds(s + RING, 1)].bitcast(U32)).then_inc(m.gid, 1)

            def weighted(s, r, added):
                v.wait_ge(m.down, s + (NSH + 1))
                if not isinstance(added, int) or added > 0:
                    v.wait_ge(m.add[r % 2], added)
                v.tensor_copy(aidx[:, r:r + 1].bitcast(U32),
                              slot_row[:, bass.ds(s, 1)].bitcast(U32))
                v.wait_ge(m.gid, s + (RING + 1))
                v.tensor_scalar(y_sb[:, r], Y[r % 2][:, 0:DIM], meta[:, r:r + 1], None, ALU.mult
                                ).then_inc(m.y, 1)

            def step(grp, r):
                s = grp * RING + r
                first = isinstance(grp, int) and grp == 0
                if not first or r >= 1:
                    hidden_T(s + (NSH - 1), (r - 1) % RING, False)
                if not first or r >= 2:
                    weighted(s - 2, (r - 2) % RING,
                             grp * 32 - (16 if r >= 2 else 32))
                keep(s, r, first)
                hidden(s + NSH, r, False)

            for grp in range(2):
                for r in range(RING):
                    step(grp, r)
            with v.Fori(2, later + 1) as grp:
                for r in range(RING):
                    step(grp, r)
            last = later * RING + RING
            weighted(last - 2, RING - 2, later * 32 + 16)
            hidden_T(last + (NSH - 1), RING - 1, False)
            weighted(last - 1, RING - 1, later * 32 + 16)
            for t in range(0, NT, CHUNK):
                v.wait_ge(m.sum_ld[t // CHUNK], 32)
                v.tensor_tensor(x_res[:, t:t + CHUNK, :], x_res[:, t:t + CHUNK, :],
                                acc_b[:, t:t + CHUNK, :], ALU.add).then_inc(m.x, 1)
                if m.c == 0:
                    v.wait_ge(m.x, t // CHUNK + 1)
                    for tt in range(t, t + CHUNK):
                        ins = v.bn_stats(a_stats[:, tt, :], x_res[:, tt, :])
            if m.c == 0:
                ins.then_inc(m.x, 1)
                v.wait_ge(m.x, NT // CHUNK + 1)

        def attention_vector(v):
            U, PJ, SC, PT, O, X = bank[4:6], bank[0:4], bank[0:2], bank[2:4], bank[4:6], bank[6:8]
            v.memset(vx[:, :, :, HD:HD + 1], 1.0).then_inc(a["ones"], 1)
            n_chain = [0]

            def link(ins):
                n_chain[0] += 1
                ins.then_inc(a["chain"], 1)
                v.wait_ge(a["chain"], n_chain[0])

            v.wait_ge(s_load, 48)
            layer_norm_stats(v, link, a["var"], a["std"], a_stats, a_mv, a_rstd)
            for b in range(BATCHES):
                for t in range(TB):
                    tt = b * TB + t
                    v.tensor_scalar(xn[:, t, :], x_res[:, tt, :], a_mv[:, tt, 0:1],
                                    a_rstd[:, tt:tt + 1],
                                    ALU.subtract, ALU.mult).then_inc(a["norm"], 1)
                for t in range(TB):
                    v.wait_ge(a["u"], TB * b + t + 1)
                    v.wait_ge(a["norm"], TB * b + t + 1)
                    for i, width in enumerate((QD, KVD)):
                        ins = v.tensor_tensor_reduce((xq, xk)[i][:, t, :], xn[:, t, :],
                                                     U[t % 2][:, i * DIM:(i + 1) * DIM],
                                                     1.0 / width, 0.0, ALU.mult, ALU.add,
                                                     a_ss[:, t, i:i + 1])
                    ins.then_inc(a["ss"], 1)
                v.wait_ge(a["ss"], TB * (b + 1))
                v.tensor_scalar(a_r[:, :, :], a_ss[:, :, :], RMS_EPS, None, ALU.add
                                ).then_inc(a["var"], 1)
                v.wait_ge(a["std"], b + 2)
                link(v.reciprocal(a_r[:, :, :], a_r[:, :, :]))
                for t in range(TB):
                    v.tensor_scalar(xq[:, t, :], xn[:, t, :], a_r[:, t, 0:1],
                                    -float(HD) ** -0.5, ALU.mult, ALU.mult
                                    ).then_inc(a["scaled"], 1)
                    v.tensor_scalar(xk[:, t, :], xn[:, t, :], a_r[:, t, 1:2], None, ALU.mult
                                    ).then_inc(a["scaled"], 1)
                for i in range(1, TB, 2):
                    v.wait_ge(a["pj"], 24 * b + i + 1)
                    v.tensor_copy(vx[:, i, :, 0:HD], PJ[i][:, :].rearrange(
                        "p (g d) -> p g d", g=KVH)).then_inc(a["pj_dve"], 1)
                for i in range(KC + QC):
                    v.wait_ge(a["hi"], (KC + QC) * b + i + 1)
                    if i >= KC + 4:
                        v.wait_ge(a_moved[i % 4], 8 * (KC + QC) * b + 32 * (i // 4))
                    for half in range(2):
                        mine = slice(HD * half, HD * (half + 1))
                        if i < KC:
                            hi, w = kT[mine, 2 * i + half, 0], kn[mine, i:i + 1]
                            dst = kT[mine, 2 * i + half, 1]
                        else:
                            hi, w = qT[mine, i - KC, half], qn[mine, i - KC:i - KC + 1]
                            dst = q_low[mine, i % 4]
                        ins = v.scalar_tensor_tensor(out=dst, in0=PJ[i % 4][mine, :], scalar=w,
                                                     in1=hi, op0=ALU.mult, op1=ALU.subtract)
                    ins.then_inc(a["lo"], 1)
                N = PAIRS * b

                def biased(n):
                    t, g, pr = n // 16, n // 2 % KVH, n % 2
                    c0 = 0 if t else P
                    v.wait_ge(a["s"], N + n + 1)
                    if n >= 2:
                        v.wait_ge(a["p"], N + n - 1)
                    for hh in range(2):
                        h = REP * g + 2 * pr + hh
                        v.tensor_tensor_reduce(scores[:, n % 2, hh, c0:2 * P],
                                               nbias[:, h, c0:2 * P],
                                               SC[n % 2][:, hh * 2 * P + c0:(hh + 1) * 2 * P],
                                               1.0, 3e38, ALU.add, ALU.min,
                                               low[:, n % 2, hh:hh + 1]).then_inc(a["low"], 1)

                v.wait_ge(a["bias"], 1)
                biased(0)
                for n in range(PAIRS + 1):
                    if n + 1 < PAIRS:
                        biased(n + 1)
                    if n % 2 == 1:
                        v.wait_ge(a["pt"], N + n + 1)
                        if n >= 2:
                            v.wait_ge(a["pv"], N + n - 1)
                        k0 = 0 if n // 16 else 1
                        v.tensor_copy(probT[:, 1, :, k0:2, :], PT[1][:, :].rearrange(
                            "p (h k q) -> p h k q", h=2, k=2)[:, :, k0:2, :]
                            ).then_inc(a["pt_dve"], 1)
                    if n >= 2 and n % 2 == 0:
                        u = n // 2 - 1
                        t, g = u // KVH, u % KVH
                        v.wait_ge(a["pv"], N + n)
                        if g == 0 and t >= 2:
                            v.wait_ge(a["ot"], 16 * b + 4 * (t - 1))
                        o = O[u % 2][:, 0:REP * (HD + 1)].rearrange("p (r d) -> p r d", r=REP)
                        link(v.reciprocal(osum[:, :], o[:, :, HD]))
                        v.tensor_tensor(heads_o[:, t % 2, g * REP * HD:(g + 1) * REP * HD]
                                        .rearrange("p (r d) -> p r d", r=REP), o[:, :, 0:HD],
                                        osum.unsqueeze(2).broadcast_to([P, REP, HD]), ALU.mult
                                        ).then_inc(a["on"], 1)
                    if (n % 16 == 2 and n > 16) or n == PAIRS:
                        t = n // 16 - 1
                        v.wait_ge(a["y"], TB * b + t + 1)
                        v.tensor_tensor(x_res[:, b * TB + t, :], X[0][:, 0:DIM],
                                        x_res[:, b * TB + t, :], ALU.add).then_inc(a["res"], 1)
            v.wait_ge(a["res"], NT)

        @block.vector
        def _(v):
            moe_vector(v, moe[0])
            attention_vector(v)
            moe_vector(v, moe[1])


def kernel(**inputs):
    import numpy as np
    import concourse.bacc as bacc
    from concourse.bass_utils import run_bass_kernel_spmd as run

    def f(n):
        return np.asarray(inputs[n])

    c = np.ascontiguousarray

    def by_rows(w):
        return c(w.reshape(w.shape[0] // P, P, w.shape[1]).transpose(1, 0, 2))

    wq, wk, wv, wo = (f("L0_attn_" + n) for n in ("wq", "wk", "wv", "wo"))
    order = [REP * (2 * j + half) + r for j in range(KVH // 2) for r in range(REP)
             for half in range(2)]
    wqp = wq.reshape(HEADS, HD, DIM)[order].reshape(QD, DIM)
    qnp = f("L0_attn_q_norm_w").reshape(HEADS, HD)[order].reshape(QC, P)
    gu = f("L0_ffn_w_gate_up")
    dn = f("L0_ffn_w_down")
    sgu = f("L0_ffn_ws_gate_up").reshape(2, 2, FFN, DIM).transpose(1, 0, 2, 3).reshape(
        2, 2 * FFN, DIM)
    sdn = f("L0_ffn_ws_down")
    arrays = {
        "x": c(f("L0_attn_x").reshape(TOKENS, DIM)),
        "gate": by_rows(f("L0_ffn_gate_w").T),
        "wgu": c(gu.transpose(0, 2, 1).reshape(NE, KD, P, 2 * FFN).transpose(0, 2, 1, 3)),
        "wdn": c(dn.transpose(0, 2, 1).reshape(NE, 2, FC, DIM).transpose(0, 2, 1, 3)),
        "sgu": c(sgu.transpose(0, 2, 1).reshape(2, KD, P, 2 * FFN).transpose(0, 2, 1, 3)),
        "sdn": c(sdn.T.reshape(2, 2, FC, DIM).transpose(0, 2, 1, 3)),
        "wq": by_rows(wqp.T),
        "wqn": by_rows(wq),
        "wk": by_rows(wk.T),
        "wkn": by_rows(wk),
        "wv": by_rows(wv.T),
        "wo": by_rows(wo.T),
        "qn": c(qnp.T),
        "kn": c(f("L0_attn_k_norm_w").reshape(KC, P).T),
    }
    nc = bacc.Bacc("TRN2", target_bir_lowering=False, num_devices=1)
    args = [nc.dram_tensor(f"in_{n}", v.shape, mybir.dt.from_np(v.dtype),
                           kind="ExternalInput").ap() for n, v in arrays.items()]
    args.append(nc.dram_tensor("out", (TOKENS, DIM), F32, kind="ExternalOutput").ap())
    macaron(nc, *args)
    r = run(nc, [{f"in_{n}": v for n, v in arrays.items()}], core_ids=[0])
    return r.results[0]["out"].reshape(inputs["L0_attn_x"].shape)
```

```python
from contextlib import ExitStack

import concourse.bass as bass
from concourse import mybir

F32 = mybir.dt.float32
BF16 = mybir.dt.bfloat16
F16 = mybir.dt.float16
I32 = mybir.dt.int32
U32 = mybir.dt.uint32
ALU = mybir.AluOpType
ACT = mybir.ActivationFunctionType
AX = mybir.AxisListType

P = 128
DIM = 256
KD = DIM // P
TOKENS = 1024
NT = TOKENS // P
BATCHES = 2
TB = NT // BATCHES
LN_PARTS = ([list(range(TB)), list(range(TB, NT))], [list(range(NT - 1)), [NT - 1]])
CHUNK = 2
NE = 64
TOPK = 6
FFN = 176
FC = FFN // 2
RING = 4
ROW = DIM + NE
MAX_EXTRA = 48
MAX_BLOCKS = NE + MAX_EXTRA
NSH = 2 * NT
HEADS = 32
KVH = 8
HD = 64
REP = HEADS // KVH
QD = HEADS * HD
KVD = KVH * HD
QC = QD // P
KC = KVD // P
WINDOW = 128
MASKED = 1e34
W_SCALE = 64.0
ALIBI_RATIO = 2.0 ** (-8.0 / HEADS)
PAIRS = TB * KVH * 2
LN_EPS, RMS_EPS, TOPK_EPS = 1e-5, 1e-6, 1e-20


def macaron(nc, x_in, gate_in, wgu_in, wdn_in, sgu_in, sdn_in, wq_in, wqn_in, wk_in, wkn_in,
            wv_in, wo_in, qn_in, kn_in, out):
    ctx = ExitStack()
    with ctx:
        def sb(name, shape, dt=F32):
            return ctx.enter_context(nc.sbuf_tensor(name, shape, dt))

        def sem(name):
            return ctx.enter_context(nc.semaphore(name))

        bank = [ctx.enter_context(nc.psum_tensor(f"bank{i}", [P, 512], F32)) for i in range(8)]

        table_x = [nc.dram_tensor(f"table_x{c}", (P + TOKENS, ROW), F32).ap() for c in range(2)]
        acc = [[nc.dram_tensor(f"acc{c}{a}", (P + TOKENS, DIM), F32).ap() for a in range(2)]
               for c in range(2)]

        x_res = sb("x_res", [P, NT, DIM])
        ident = sb("ident", [P, P])
        before = sb("before", [P, P], BF16)
        ones = sb("ones", [P, P], BF16)
        iota_e = sb("iota_e", [P, NE])
        slot0 = sb("slot0", [P, NE])
        ones_e = sb("ones_e", [P, NE])
        x_stats = sb("x_stats", [P, NT, 6])
        steps_blk = sb("steps_blk", [P, 7])
        steps_grp = sb("steps_grp", [P, 12])
        iota_p = sb("iota_p", [P, 1])
        iota_i = sb("iota_i", [P, P], I32)
        iota_r = sb("iota_r", [P, P])
        row_id = sb("row_id", [P, NT])
        zeros = sb("zeros", [P, ROW])
        stage = sb("stage", [P, 2 * P])
        gate_w = sb("gate_w", [P, KD, NE])
        wq = sb("wq", [P, 2, KD, QD], F16)
        wk = sb("wk", [P, 2, KD, KVD], F16)
        wv = sb("wv", [P, KD, KVD])
        rows_or_wo = sb("rows_or_wo", [P, QC * DIM])
        wq_rows = rows_or_wo[:, :].rearrange("p (c n) -> p c n", n=DIM)
        wo = rows_or_wo[:, :].bitcast(F16).rearrange("p (a c n) -> p a c n", a=2, n=DIM)
        wk_rows = wv[:, :, :].rearrange("p k (a n) -> p (k a) n", n=DIM)
        gram = sb("gram", [P, KD, 2, DIM])
        qn = sb("qn", [P, QC])
        kn = sb("kn", [P, KC])
        dist = sb("dist", [P, 2 * P])

        ARENA = 33472
        arena = sb("arena", [P, ARENA])
        used = [0]

        def take(*shape):
            n = 1
            for s in shape:
                n *= s
            v = arena[:, used[0]:used[0] + n]
            used[0] += n
            assert used[0] <= ARENA, used[0]
            names = [f"d{i}" for i in range(len(shape))]
            return v.rearrange(f"p ({' '.join(names)}) -> p {' '.join(names)}",
                               **dict(zip(names, shape))) if len(shape) > 1 else v

        rows = take(NT, ROW)
        xT = take(KD, TOKENS)
        w_gu = take(RING, KD, 2 * FFN)
        w_dn = take(RING, 2, DIM)
        ws_gu = take(2, KD, 2 * FFN)
        ws_dn = take(2, 2, DIM)
        blkT = take(2, KD, P)
        silu = take(2, FFN)
        up = take(2, FFN)
        hid = take(2, FFN)
        hidT = take(2, 2, P)
        meta = take(RING)
        gidx = take(RING)
        aidx = take(RING)
        shared_y = take(NT, DIM)
        onehot = take(NT * TOPK * NE // 2).bitcast(BF16).rearrange("p (c e) -> p c e", e=NE)
        pair_sum = take(NT * 3 * NE // 2).bitcast(BF16).rearrange("p (t k e) -> p t k e", k=3, e=NE)
        routing0 = used[0]
        at_slot = take(NT * TOPK * P // 2).bitcast(F16).rearrange("p (c r) -> p c r", r=P)
        at_block = take(NT * TOPK * MAX_BLOCKS // 2).bitcast(F16).rearrange(
            "p (c n) -> p c n", n=MAX_BLOCKS)
        routing1 = used[0]
        used[0] = routing0
        onehot_slot = take(NT * TOPK, NE)
        used[0] = routing0
        blk = take(RING, ROW)
        y_sb = take(RING, DIM)
        used[0] = routing0
        acc_b = take(NT, DIM)
        used[0] = routing1
        wq32 = take(KD, QD)
        wk32 = shared_y.rearrange("p t n -> p (t n)")[:, 0:KD * KVD].rearrange(
            "p (k n) -> p k n", k=KD)
        probs = take(NT, NE)
        slotm = take(NT, NE)
        pos2 = take(NT, NE)
        sel_used = take(NT * NE // 2)
        sel = sel_used.bitcast(BF16).rearrange("p (t e) -> p t e", e=NE)
        top_v = take(NT, 8)
        top_i = take(NT, 8)
        top_f = take(NT, TOPK)
        slot_f = take(NT * TOPK)
        slot_u = take(NT * TOPK)
        place_u = take(2, NT * TOPK)
        place_f = take(2, NT * TOPK)
        slot_row = take(MAX_BLOCKS + RING)
        factor = take(NT)
        mv = take(NT, 2)
        rstd = take(NT)
        rmax = take(NT)
        rsum = take(NT)
        rrec = take(NT)
        wsum = take(NT)
        wrec = take(NT)
        more = take(NE, 7)
        extra = take(NE)
        extra_in = take(NE)
        base = take(NE)
        owner = take(1)
        owner_cmp = take(NE)
        grp_cmp = take(12)
        grp_f = take(1)
        table = take(MAX_BLOCKS)
        groups = take(1)
        used[0] = 0
        nbias = take(HEADS, 2 * P)
        proj0 = used[0]
        xn = take(TB, DIM)
        xq = take(TB, DIM)
        xk = take(TB, DIM)
        xnT = take(KD, TB * P)
        xqT, xkT = (take(2, KD, TB * P // 2).bitcast(F16) for _ in range(2))
        qT = take(QC, 2, TB * P // 2).bitcast(F16)
        kT = take(KVH, 2, TB * P // 2).bitcast(F16)
        wo32 = take(4, TB * P // 2)
        q_low = wo32.bitcast(F16)
        vx = take(TB, KVH, HD + 1)
        scores = take(2, 2, 2 * P)
        prob = take(2, 2, 2 * P)
        probT = take(2, 2, 2, P)
        heads_o = arena[:, proj0:proj0 + 2 * QD].rearrange("p (b n) -> p b n", b=2)
        headsT = arena[:, proj0 + 2 * QD:proj0 + 3 * QD].bitcast(F16).rearrange(
            "p (a c n) -> p a c n", a=2, n=P)
        low = take(2, 2)
        osum = take(REP)
        a_mv = take(NT, 2)
        a_rstd = take(NT)
        a_ss = take(TB, 2)
        a_r = take(TB, 2)

        s_x = [sem("s_x0"), sem("s_x1")]
        s_const = sem("s_const")
        s_fix = sem("s_fix")
        s_load = sem("s_load")
        s_attw = sem("s_attw")
        s_rows_w = sem("s_rows_w")
        s_wv = sem("s_wv")
        s_wo = sem("s_wo")
        s_gram_mm = sem("s_gram_mm")
        s_gram = sem("s_gram")
        s_out = sem("s_out")

        class Moe:
            def __init__(m, c):
                def s(n):
                    return sem(f"m{c}_{n}")
                m.c = c
                m.chain = s("chain")
                m.var = s("var")
                m.std = s("std")
                m.norm = s("norm")
                m.tr = s("tr")
                m.tr_sb = s("tr_sb")
                m.logits = s("logits")
                m.shifted = s("shifted")
                m.expd = s("expd")
                m.sel = s("sel")
                m.rank = s("rank")
                m.onehots = s("onehots")
                m.scaled = s("scaled")
                m.ids = s("ids")
                m.asked = s("asked")
                m.gid = s("gid")
                m.owner = s("owner")
                m.ownerT = s("ownerT")
                m.table = s("table")
                m.comb = s("comb")
                m.tab = s("tab")
                m.wsh = s("wsh")
                m.w_gu = [s(f"w_gu{r}") for r in range(RING)]
                m.w_dn = [s(f"w_dn{r}") for r in range(RING)]
                m.blk = [s(f"blk{r}") for r in range(RING)]
                m.gu = s("gu")
                m.silu = s("silu")
                m.hid = s("hid")
                m.half = s("half")
                m.hT = s("hT")
                m.hT_sb = s("hT_sb")
                m.down = s("down")
                m.ysh = s("ysh")
                m.y = s("y")
                m.seed = s("seed")
                m.add = [s(f"add{a}") for a in range(2)]
                m.sum_ld = [s(f"sum_ld{i}") for i in range(NT // CHUNK)]
                m.x = s("x")

        moe = [Moe(0), Moe(1)]
        a = {n: sem(f"a_{n}") for n in (
            "chain", "norm", "tr", "tr_sb", "u", "scaled", "pj", "pj_act", "pj_dve", "hi", "lo", "s", "low",
            "whi", "wlo", "xhi", "xlo",
            "wohi", "wolo", "ot_lo",
            "p", "pt", "pt_act", "pt_dve", "pv", "on", "ot", "ot_sb", "y", "res", "ones", "bias", "var", "std",
            "ss")}

        a_moved = [sem(f"a_moved{i}") for i in range(4)]

        block = ctx.enter_context(nc.Block())
        TR, GU, HT, Y = bank[0:2], bank[2:4], bank[4:6], bank[6:8]
        LOGITS, RANK, COUNT, IDS, OWNER = bank[6], bank[1], bank[0], bank[1], bank[0]
        IDS0, OWNER0 = 0, P

        WEIGHTS = [((wq[:, 0, k, :], wq[:, 1, k, :]), wq32[:, k, :]) for k in range(KD)]
        WEIGHTS.append(((wk[:, 0], wk[:, 1]), wk32))
        N_CONST = 1
        SPLIT = 15
        SCALE_AT = 12
        TURN_AT, LOW_AT = range(1, 9, 2), range(2, 10, 2)
        OUT_AT = range(5, 13)
        RANKS_AT = 4

        def turn_bank(t, i):
            return bank[(6, 2, 3, 0)[i] if t == TB - 1 else 6]

        def moe_sync(sp, m):
            c = m.c
            for r in range(2):
                sp.dma_start(ws_gu[:, r], sgu_in[r]).then_inc(m.wsh, 16)
                sp.dma_start(ws_dn[0:FC, r], sdn_in[r]).then_inc(m.wsh, 16)
            for r in range(RING):
                sp.dma_start(w_gu[:, r], wgu_in[r]).then_inc(m.w_gu[r], 16)
                sp.dma_start(w_dn[0:FC, r], wdn_in[r]).then_inc(m.w_dn[r], 16)
            if c == 0:
                sp.dma_start(wq_rows[:, :, :], wqn_in).then_inc(s_rows_w, 16)
                sp.dma_start(wk_rows, wkn_in).then_inc(s_rows_w, 16)
                sp.dma_start(wq32, wq_in).then_inc(s_attw, 16)
            sp.dma_start(table_x[c][0:P, :], zeros[:, :]).then_inc(m.tab, 16)
            sp.dma_start(acc[c][1][P:, :].rearrange("(t p) n -> p t n", p=P),
                         zeros[:, 0:DIM].unsqueeze(1).broadcast_to([P, NT, DIM])
                         ).then_inc(m.seed, 16)
            for k in range(2):
                sp.dma_start(acc[c][k][0:P, :], zeros[:, 0:DIM]).then_inc(m.seed, 16)
            sp.wait_ge(m.comb, 1)
            sp.dma_start(table_x[c][P:, :].rearrange("(t p) n -> p t n", p=P), rows
                         ).then_inc(m.tab, 16)
            sp.wait_ge(m.ysh, NT)
            sp.dma_start(acc[c][0][P:, :].rearrange("(t p) n -> p t n", p=P),
                         shared_y).then_inc(m.seed, 16)
            if c == 0:
                sp.wait_ge(m.seed, 64)
                sp.dma_start(wk32, wk_in).then_inc(s_attw, 16)
            sp.wait_ge(m.table, 2)
            later = sp.value_load(groups[0:1, 0:1].bitcast(I32), min_val=NE // RING - 1,
                                 max_val=MAX_BLOCKS // RING - 1)
            with sp.Fori(1, later + 1) as grp:
                for r in range(RING):
                    s = grp * RING + r
                    expert = sp.value_load(table[0:1, bass.ds(s, 1)].bitcast(I32), min_val=0,
                                           max_val=NE - 1)
                    sp.wait_ge(m.gu, s + (NSH - RING + 1))
                    sp.dma_start(w_gu[:, r], wgu_in[bass.ds(expert, 1)].rearrange(
                        "o p k n -> (o p) k n")).then_inc(m.w_gu[r], 16)
                    sp.wait_ge(m.down, s + (NSH - RING + 1))
                    sp.dma_start(w_dn[0:FC, r], wdn_in[bass.ds(expert, 1)].rearrange(
                        "o p k n -> (o p) k n")).then_inc(m.w_dn[r], 16)
            for k in range(2):
                sp.wait_ge(m.add[k], later * 32 + 32)
            for t in range(0, NT, CHUNK):
                for k, dst in enumerate((x_res, acc_b)):
                    sp.dma_start(dst[:, t:t + CHUNK, :], acc[c][k][P * (t + 1):P * (t + CHUNK + 1), :]
                                 .rearrange("(t p) n -> p t n", p=P)).then_inc(m.sum_ld[t // CHUNK],
                                                                               16)

            if c == 0:
                sp.wait_ge(s_gram_mm, 1)
                sp.dma_start(wv[:, :, :], wv_in).then_inc(s_wv, 16)

        @block.sync
        def _(sp):
            for i in range(2):
                part = slice(LN_PARTS[0][i][0], LN_PARTS[0][i][-1] + 1)
                sp.dma_start(x_res[:, part, :],
                             x_in.rearrange("(t p) n -> p t n", p=P)[:, part, :]
                             ).then_inc(s_x[i], 16)
            sp.dma_start(gate_w[:, :, :], gate_in).then_inc(s_load, 16)
            sp.dma_start(qn[:, :], qn_in).then_inc(s_load, 16)
            sp.dma_start(kn[:, :], kn_in).then_inc(s_load, 16)
            sp.wait_ge(s_const, N_CONST)
            moe_sync(sp, moe[0])
            for b in range(BATCHES):
                for i in range(KC + QC):
                    sp.wait_ge(a["lo"], (KC + QC) * b + i + 1)
                    for half in range(2):
                        mine = slice(HD * half, HD * (half + 1))
                        other = slice(HD * (1 - half), HD * (2 - half))
                        if i < KC:
                            dst, src = kT[other, 2 * i + half], kT[mine, 2 * i + half]
                        else:
                            dst, src = qT[other, i - KC, half], q_low[mine, i % 4]
                        sp.dma_start(dst, src).then_inc(a_moved[i % 4], 16)
                if b == 0:
                    for i in range(4):
                        sp.wait_ge(a_moved[i], 8 * (KC + QC))
                    for i in range(4):
                        if i:
                            sp.wait_ge(a["wolo"], i)
                        sp.dma_start(wo32, wo_in[:, 4 * i:4 * i + 4, :]).then_inc(s_wo, 16)
            sp.wait_ge(a["res"], NT)
            moe_sync(sp, moe[1])
            for t in range(0, NT, CHUNK):
                sp.wait_ge(moe[1].x, t // CHUNK + 1)
                sp.dma_start(out[t * P:(t + CHUNK) * P, :].rearrange("(t p) n -> p t n", p=P),
                             x_res[:, t:t + CHUNK, :]).then_inc(s_out, 16)
            sp.wait_ge(s_out, 16 * (NT // CHUNK))

        def moe_gpsimd(g, m):
            c = m.c
            def waited():
                g.sem_inc(m.asked, 1)

            def gather(r):
                g.indirect_dma_start(
                    out=blk[:, r], out_offset=None, in_=table_x[c],
                    in_offset=bass.IndirectOffsetOnAxis(ap=gidx[:, r:r + 1].bitcast(U32), axis=0)
                    ).then_inc(m.blk[r], 16)

            def add_rows(r):
                g.indirect_dma_start(
                    out=acc[c][r % 2],
                    out_offset=bass.IndirectOffsetOnAxis(ap=aidx[:, r:r + 1].bitcast(U32), axis=0),
                    in_=y_sb[:, r], in_offset=None, compute_op=ALU.add).then_inc(m.add[r % 2], 16)

            for q in range(NSH + 2):
                if q == SPLIT:
                    g.wait_ge(m.tab, 32)
                    g.wait_ge(m.gid, RING)
                    for r in range(RING):
                        gather(r)
                if q >= 2 and q % 2 == 1:
                    t = (q - 2) // 2
                    g.wait_ge(m.half, t + 1)
                    g.tensor_tensor(shared_y[:, t, :], shared_y[:, t, :], x_res[:, t, :], ALU.add
                                    ).then_inc(m.ysh, 1)
                if q < SPLIT:
                    g.wait_ge(m.silu, q + 1)
                    if q >= 2:
                        g.wait_ge(m.hT, q - 1)
                    g.tensor_tensor(hid[:, q % 2, :], silu[:, q % 2, :], up[:, q % 2, :],
                                    ALU.mult).then_inc(m.hid, 1)
            g.wait_ge(m.table, 2)
            later = g.value_load(groups[0:1, 0:1].bitcast(I32), min_val=NE // RING - 1,
                                 max_val=MAX_BLOCKS // RING - 1)
            g.wait_ge(m.seed, 64)

            def serve(grp, r, first):
                g.wait_ge(m.gid, grp * RING + (r + 1))
                if not first:
                    waited()
                gather(r)
                g.wait_ge(m.y, grp * RING + (r - RING + 1))
                if not first:
                    g.wait_ge(m.add[r % 2], grp * 32 + (16 * (r // 2) - 32))
                    waited()
                elif r >= 2:
                    g.wait_ge(m.add[r % 2], 16)
                add_rows(r)

            for r in range(RING):
                serve(1, r, True)
            with g.Fori(2, later + 1) as grp:
                for r in range(RING):
                    serve(grp, r, False)
            for r in range(RING):
                g.wait_ge(m.y, later * RING + (r + 1))
                g.wait_ge(m.add[r % 2], later * 32 + 16 * (r // 2))
                waited()
                add_rows(r)

        @block.gpsimd
        def _(g):
            n = [0]

            def fix(ins):
                n[0] += 1
                ins.then_inc(s_fix, 1)
                g.wait_ge(s_fix, n[0])

            fix(g.memset(ident[:, :], 0.0))
            fix(g.affine_select(out=ident[:, :], in_=ident[:, :], compare_op=ALU.not_equal,
                                fill=1.0, base=0, pattern=[[-1, P]], channel_multiplier=1))
            fix(g.memset(ones[:, :], 1.0))
            fix(g.affine_select(out=before[:, :], in_=ones[:, :], compare_op=ALU.is_gt,
                                fill=0.0, base=0, pattern=[[1, P]], channel_multiplier=-1))
            fix(g.iota(iota_i[:, 0:NE], pattern=[[1, NE]], base=0, channel_multiplier=0))
            fix(g.tensor_copy(iota_e[:, :], iota_i[:, 0:NE]))
            fix(g.iota(iota_i[:, 0:NE], pattern=[[P, NE]], base=0, channel_multiplier=0))
            fix(g.tensor_copy(slot0[:, :], iota_i[:, 0:NE]))
            fix(g.iota(iota_i[:, 0:7], pattern=[[P, 7]], base=P, channel_multiplier=0))
            fix(g.tensor_copy(steps_blk[:, :], iota_i[:, 0:7]))
            fix(g.iota(iota_i[:, 0:12], pattern=[[RING, 12]], base=0, channel_multiplier=0))
            fix(g.tensor_copy(steps_grp[:, :], iota_i[:, 0:12]))
            fix(g.iota(iota_i[:, 0:1], pattern=[[1, 1]], base=0, channel_multiplier=1))
            fix(g.tensor_copy(iota_p[:, :], iota_i[:, 0:1]))
            fix(g.memset(ones_e[:, :], 1.0))
            fix(g.memset(zeros[:, :], 0.0))
            fix(g.iota(iota_i[:, :], pattern=[[1, P]], base=0, channel_multiplier=0))
            fix(g.tensor_copy(iota_r[:, :], iota_i[:, :]))
            fix(g.iota(iota_i[:, 0:NT], pattern=[[P, NT]], base=P, channel_multiplier=1))
            fix(g.tensor_copy(row_id[:, :], iota_i[:, 0:NT]))
            g.memset(iota_i[:, 0:1], 0).then_inc(s_const, 1)
            dist_i = stage[:, :].bitcast(I32)
            fix(g.iota(dist_i, pattern=[[-1, 2 * P]], base=P, channel_multiplier=1))
            fix(g.tensor_copy(dist[:, :], dist_i))
            fix(g.affine_select(out=dist[:, :], in_=dist[:, :], compare_op=ALU.is_ge, fill=MASKED,
                                base=P, pattern=[[-1, 2 * P]], channel_multiplier=1))
            fix(g.affine_select(out=dist[:, :], in_=dist[:, :], compare_op=ALU.is_ge, fill=MASKED,
                                base=WINDOW - P, pattern=[[1, 2 * P]], channel_multiplier=-1))
            moe_gpsimd(g, moe[0])
            g.wait_ge(moe[0].x, NT // CHUNK)
            for h in range(HEADS):
                ins = g.tensor_scalar(nbias[:, h, :], dist[:, :], float(ALIBI_RATIO ** h), None,
                                      ALU.mult)
            ins.then_inc(a["bias"], 1)
            moe_gpsimd(g, moe[1])

        def moe_tensor(pe, m):
            for t in range(NT + 1):
                if t < NT:
                    pe.wait_ge(m.norm, t + 1)
                    if t >= 2:
                        pe.wait_ge(m.tr_sb, t - 1)
                    for k in range(KD):
                        mm = pe.transpose(TR[t % 2][:, k * P:(k + 1) * P],
                                          rows[:, t, k * P:(k + 1) * P], ident[:, :])
                    mm.then_inc(m.tr, 1)
                if t >= 1:
                    pe.wait_ge(m.tr_sb, t)
                    for k in range(KD):
                        mm = pe.matmul(LOGITS[:, (t - 1) * NE:t * NE],
                                       xT[:, k, (t - 1) * P:t * P], gate_w[:, k, :],
                                       start=(k == 0), stop=(k == KD - 1))
            mm.then_inc(m.logits, 1)

            def ranks():
                pe.wait_ge(m.sel, 1)
                for j in range(NT):
                    pe.matmul(COUNT[:, 0:NE], ones[:, :], sel[:, j, :],
                              start=(j == 0), stop=(j == NT - 1))
                for t in range(NT):
                    for j in range(t + 1):
                        mm = pe.matmul(RANK[:, t * NE:(t + 1) * NE],
                                       (before if j == t else ones)[:, :], sel[:, j, :],
                                       start=(j == 0), stop=(j == t))
                mm.then_inc(m.rank, 1)

            def gate_up(r, lhs, weights):
                for k in range(KD):
                    mm = pe.matmul(GU[r % 2][:, 0:2 * FFN], lhs(k), weights[:, k, :],
                                   start=(k == 0), stop=(k == KD - 1))
                mm.then_inc(m.gu, 1)

            def turn_hidden(q, r, first):
                pe.wait_ge(m.hid, q + 1)
                if not first:
                    pe.wait_ge(m.hT_sb, q - 1)
                for k in range(2):
                    mm = pe.transpose(HT[r % 2][0:FC, k * P:(k + 1) * P],
                                      hid[:, r % 2, k * FC:(k + 1) * FC], ident[:, :])
                mm.then_inc(m.hT, 1)

            def down(q, r, ybank, weights, start, stop):
                pe.wait_ge(m.hT_sb, q + 1)
                for k in range(2):
                    mm = pe.matmul(ybank[:, 0:DIM], hidT[0:FC, r % 2, k, :],
                                   weights[0:FC, k, :],
                                   start=(start and k == 0), stop=(stop and k == 1))
                mm.then_inc(m.down, 1)

            pe.wait_ge(m.wsh, 64)
            def slot_rows():
                for i in range(NT * TOPK):
                    if i % TOPK == 0:
                        pe.wait_ge(m.scaled, i // TOPK + 1)
                    mm = pe.matmul(IDS[:, IDS0:IDS0 + MAX_BLOCKS], at_slot[:, i, :], at_block[:, i, :],
                                   start=(i == 0), stop=(i == NT * TOPK - 1))
                mm.then_inc(m.ids, 1)
                pe.wait_ge(m.owner, 1)
                pe.transpose(OWNER[0:1, OWNER0:OWNER0 + P], owner[:, 0:1], ident[:, :]
                             ).then_inc(m.ownerT, 1)

            for q in range(NSH + 2):
                if q == RANKS_AT:
                    ranks()
                if q == SPLIT:
                    slot_rows()
                if q < NSH:
                    if q >= 2:
                        pe.wait_ge(m.hid, q - 1)
                    t = q // 2
                    gate_up(q, lambda k: xT[:, k, t * P:(t + 1) * P], ws_gu[:, q % 2])
                if q >= 2:
                    d = q - 2
                    if d == 0:
                        pe.wait_ge(m.shifted, 1)
                    if d % 2 == 0 and d >= 4:
                        pe.wait_ge(m.half, d // 2 - 1)
                    down(d, d, Y[d // 2 % 2], ws_dn[:, d % 2], d % 2 == 0, d % 2 == 1)
                if 1 <= q <= NSH:
                    turn_hidden(q - 1, q - 1, q - 1 < 2)

            pe.wait_ge(m.table, 2)
            later = pe.value_load(groups[0:1, 0:1].bitcast(I32), min_val=NE // RING - 1,
                                 max_val=MAX_BLOCKS // RING - 1)

            def step(s, r, first, grp=None):
                group = 0 if first else grp * 16
                pe.wait_ge(m.blk[r], group + 16)
                pe.wait_ge(m.tr_sb, s + (NT - 1))
                for k in range(KD):
                    mm = pe.transpose(TR[r % 2][:, k * P:(k + 1) * P],
                                      blk[:, r, k * P:(k + 1) * P], ident[:, :])
                mm.then_inc(m.tr, 1)
                if not first or r >= 2:
                    rr = (r - 2) % RING
                    pe.wait_ge(m.w_dn[rr], group + (16 if r >= 2 else 0))
                    if first:
                        pe.wait_ge(m.half, NT)
                    else:
                        pe.wait_ge(m.y, s - 3)
                    down(s + (NSH - 2), rr, Y[rr % 2], w_dn[:, rr], True, True)
                if not first or r >= 1:
                    turn_hidden(s + (NSH - 1), (r - 1) % RING, False)
                pe.wait_ge(m.w_gu[r], group + 16)
                pe.wait_ge(m.tr_sb, s + (NT + 1))
                pe.wait_ge(m.hid, s + (NSH - 1))
                gate_up(r, lambda k: blkT[:, r % 2, k, :], w_gu[:, r])

            for r in range(RING):
                step(r, r, True)
            with pe.Fori(1, later + 1) as grp:
                for r in range(RING):
                    step(grp * RING + r, r, False, grp)
            last = later * RING + RING
            for d in (2, 1):
                pe.wait_ge(m.w_dn[RING - d], later * 16 + 16)
                pe.wait_ge(m.y, last - (d + 1))
                if d == 1:
                    turn_hidden(last + (NSH - 1), RING - 1, False)
                down(last + (NSH - d), RING - d, Y[(RING - d) % 2], w_dn[:, RING - d], True, True)

        def attention_tensor(pe):
            X, U, PJ, SC, PT, O = bank[6:8], bank[4:6], bank[0:4], bank[0:2], bank[2:4], bank[4:6]
            pe.wait_ge(s_rows_w, 32)
            for i, (w, n) in enumerate(((wk_rows, KC), (wq_rows, QC))):
                for k in range(KD):
                    for j in range(n):
                        mm = pe.matmul(U[i][:, k * DIM:(k + 1) * DIM],
                                       w[:, j, k * P:(k + 1) * P], w[:, j, :],
                                       start=(j == 0), stop=(j == n - 1))
                mm.then_inc(s_gram_mm, 1)
            pe.wait_ge(s_load, 48)
            for b in range(BATCHES):
                def turn(i, src, t):
                    if i >= TB + 4:
                        pe.wait_ge(a["xlo"], 2 * TB * b + i - TB - 3)
                    elif 2 <= i < TB:
                        pe.wait_ge(a["tr_sb"], TB * b + i - 1)
                    dst = X[i % 2] if i < TB else (X + U)[(i - TB) % 4]
                    for k in range(KD):
                        mm = pe.transpose(dst[:, k * P:(k + 1) * P],
                                          src[:, t, k * P:(k + 1) * P], ident[:, :])
                    mm.then_inc(a["tr"], 1)

                for t in range(TB):
                    pe.wait_ge(a["norm"], TB * b + t + 1)
                    turn(t, xn, t)
                pe.wait_ge(s_gram, 2)
                for t in range(TB):
                    pe.wait_ge(a["tr_sb"], TB * b + t + 1)
                    if t >= 2:
                        pe.wait_ge(a["ss"], TB * b + t - 1)
                    for k in range(KD):
                        mm = pe.matmul(U[t % 2][:, :], xnT[:, k, t * P:(t + 1) * P],
                                       gram[:, k, :, :].rearrange("p a n -> p (a n)"),
                                       start=(k == 0), stop=(k == KD - 1))
                    mm.then_inc(a["u"], 1)

                def project(i):
                    if 4 <= i < 6:
                        pe.wait_ge(a["pj_act" if i % 2 == 0 else "pj_dve"], 2 * b + 1)
                    elif i >= 6:
                        pe.wait_ge(a["lo"], (KC + QC) * b + i - 5)
                    if i < 2 or i >= KC + QC + 2:
                        t = i if i < 2 else i - (KC + QC)
                        for k in range(KD):
                            mm = pe.matmul(PJ[i % 4][:, :], xnT[:, k, t * P:(t + 1) * P],
                                           wv[:, k, :], start=(k == 0), stop=(k == KD - 1))
                    else:
                        w, x, c = (wk, xkT, i - 2) if i < KC + 2 else (wq, xqT, i - 2 - KC)
                        steps = [(k, wp, xp) for wp, xp in ((0, 0), (0, 1), (1, 0))
                                 for k in range(KD)]
                        for n, (k, wp, xp) in enumerate(steps):
                            mm = pe.matmul(PJ[i % 4][:, :], w[:, wp, k, c * P:(c + 1) * P],
                                           x[:, xp, k, :], start=(n == 0),
                                           stop=(n == len(steps) - 1))
                    mm.then_inc(a["pj"], 1)

                pe.wait_ge(s_wv, 16)
                project(0)
                for t in range(TB):
                    if t == 1:
                        project(1)
                    pe.wait_ge(a["scaled"], 2 * (TB * b + t + 1))
                    turn(TB + 2 * t, xq, t)
                    turn(TB + 2 * t + 1, xk, t)
                pe.wait_ge(a["xlo"], 2 * TB * (b + 1))
                pe.wait_ge(a["wlo"], 3)
                for i in range(2, TB + KC + QC):
                    project(i)
                pe.wait_ge(a["lo"], (KC + QC) * (b + 1))
                for i in range(4):
                    pe.wait_ge(a_moved[i], 8 * (KC + QC) * (b + 1) - 32)

                N = PAIRS * b

                def score(n):
                    t, g, pr = n // 16, n // 2 % KVH, n % 2
                    if n >= 2:
                        pe.wait_ge(a["low"], 2 * (N + n - 1))
                    c0 = 0 if t else P
                    for hh in range(2):
                        c = g // 2 * REP + 2 * pr + hh
                        for part in range(2):
                            mm = pe.matmul(SC[n % 2][:, hh * 2 * P + c0:(hh + 1) * 2 * P],
                                           qT[:, c, g % 2, t * P:(t + 1) * P],
                                           kT[:, g, part, (t - 1) * P + c0:(t + 1) * P],
                                           start=(part == 0), stop=(part == 1))
                    mm.then_inc(a["s"], 1)

                def turn_probs(n):
                    t = n // 16
                    pe.wait_ge(a["p"], N + n + 1)
                    if n >= 2:
                        pe.wait_ge(a["pt_act" if n % 2 == 0 else "pt_dve"], (N + n) // 2)
                    for hh in range(2):
                        for kt in range(0 if t else 1, 2):
                            mm = pe.transpose(PT[n % 2][:, (2 * hh + kt) * P:(2 * hh + kt + 1) * P],
                                              prob[:, n % 2, hh, kt * P:(kt + 1) * P], ident[:, :])
                    mm.then_inc(a["pt"], 1)

                def values(n):
                    t, g, pr = n // 16, n // 2 % KVH, n % 2
                    u = n // 2
                    pe.wait_ge(a["pt_act" if n % 2 == 0 else "pt_dve"], (N + n) // 2 + 1)
                    if pr == 0 and u >= 2:
                        pe.wait_ge(a["on"], N // 2 + u - 1)
                    for hh in range(2):
                        r = 2 * pr + hh
                        for kt in range(0 if t else 1, 2):
                            mm = pe.matmul(O[u % 2][:, r * (HD + 1):(r + 1) * (HD + 1)],
                                           probT[:, n % 2, hh, kt, :], vx[:, t - 1 + kt, g, :],
                                           start=(kt == (0 if t else 1)), stop=(kt == 1))
                    mm.then_inc(a["pv"], 1)

                def turn_heads(t, i):
                    if i == 0:
                        pe.wait_ge(a["on"], N // 2 + KVH * (t + 1))
                    elif t < TB - 1:
                        pe.wait_ge(a["ot_lo"], 16 * b + 4 * t + i)
                    for j in range(4):
                        mm = pe.transpose(turn_bank(t, i)[:, j * P:(j + 1) * P],
                                          heads_o[:, t % 2, (4 * i + j) * P:(4 * i + j + 1) * P],
                                          ident[:, :])
                    mm.then_inc(a["ot"], 1)

                def out_step(t, i):
                    if i == 0:
                        pe.wait_ge(a["wolo"], 4)
                        if t > 0:
                            pe.wait_ge(a["res"], TB * b + t)
                    pe.wait_ge(a["ot_lo"], 16 * b + 4 * t + i // 2 + 1)
                    for j in range(2 * i, 2 * i + 2):
                        for hp, wp in ((0, 0), (0, 1), (1, 0)):
                            mm = pe.matmul(bank[7][:, 0:DIM], headsT[:, hp, j, :], wo[:, wp, j, :],
                                           start=(j == 0 and hp == wp == 0),
                                           stop=(j == QC - 1 and hp == 1))
                    if i == 7:
                        mm.then_inc(a["y"], 1)

                score(0)
                score(1)
                pe.wait_ge(a["pj_act"], 2 * (b + 1))
                pe.wait_ge(a["pj_dve"], 2 * (b + 1))
                for n in range(PAIRS + 1):
                    if n < PAIRS:
                        turn_probs(n)
                    if n + 2 == 2 * (KVH - 2):
                        for i in range(4):
                            pe.wait_ge(a_moved[i], 8 * (KC + QC) * (b + 1))
                    if n + 2 < PAIRS:
                        score(n + 2)
                    if n >= 1:
                        values(n - 1)
                    if n > 16 and n % 16 in TURN_AT:
                        turn_heads(n // 16 - 1, TURN_AT.index(n % 16))
                    if n > 16 and n % 16 in OUT_AT:
                        out_step(n // 16 - 1, OUT_AT.index(n % 16))
                for i in range(4):
                    turn_heads(TB - 1, i)
                for i in range(8):
                    out_step(TB - 1, i)
                pe.wait_ge(a["res"], TB * (b + 1))

        @block.tensor
        def _(pe):
            pe.wait_ge(s_const, N_CONST)
            pe.wait_ge(s_load, 48)
            moe_tensor(pe, moe[0])
            attention_tensor(pe)
            moe_tensor(pe, moe[1])

        def moe_scalar(act, m):
            def root(i):
                part = slice(LN_PARTS[m.c][i][0], LN_PARTS[m.c][i][-1] + 1)
                act.wait_ge(m.var, i + 1)
                nc.scalar.activation(rstd[:, part], rstd[:, part], ACT.Sqrt).then_inc(m.std, 1)

            root(0)
            for t in range(NT):
                if t == TB - 1:
                    root(1)
                act.wait_ge(m.tr, t + 1)
                nc.scalar.copy(xT[:, :, t * P:(t + 1) * P],
                               TR[t % 2][:, 0:DIM].rearrange("p (k n) -> p k n", k=KD)
                               ).then_inc(m.tr_sb, 1)
            act.wait_ge(m.shifted, 1)
            nc.scalar.activation(probs[:, :, :], probs[:, :, :], ACT.Exp).then_inc(m.expd, 1)

            def gated(q, r, first, shared=False):
                act.wait_ge(m.gu, q + 1)
                if not first:
                    act.wait_ge(m.hid, q - 1)
                if shared:
                    nc.scalar.copy(up[:, r % 2, :], GU[r % 2][:, FFN:2 * FFN])
                nc.scalar.activation(silu[:, r % 2, :], GU[r % 2][:, 0:FFN], ACT.Silu
                                     ).then_inc(m.silu, 1)

            def scale_blocks(t):
                act.wait_ge(m.onehots, t + 1)
                ch = slice(t * TOPK, (t + 1) * TOPK)
                nc.scalar.activation(at_block[:, ch, :], at_block[:, ch, :], ACT.Copy,
                                     scale=row_id[:, t:t + 1]).then_inc(m.scaled, 1)

            for q in range(NSH + 2):
                if SCALE_AT <= q < SPLIT:
                    scale_blocks(q - SCALE_AT)
                if q == SPLIT:
                    for t in range(SPLIT - SCALE_AT, NT):
                        scale_blocks(t)
                if q < NSH:
                    gated(q, q, q < 2, q < SPLIT)
                if q >= 2 and q % 2 == 1:
                    t = (q - 2) // 2
                    act.wait_ge(m.down, 2 * t + 2)
                    nc.scalar.mul(shared_y[:, t, :], Y[t % 2][:, 0:DIM], 0.5).then_inc(m.half, 1)
                if not 1 <= q <= NSH:
                    continue
                p = q - 1
                act.wait_ge(m.hT, p + 1)
                if p >= 2:
                    act.wait_ge(m.down, p - 1)
                nc.scalar.copy(hidT[0:FC, p % 2], HT[p % 2][0:FC, 0:2 * P].rearrange(
                    "p (k n) -> p k n", k=2)).then_inc(m.hT_sb, 1)
            act.wait_ge(m.table, 2)
            later = act.value_load(groups[0:1, 0:1].bitcast(I32), min_val=NE // RING - 1,
                                 max_val=MAX_BLOCKS // RING - 1)

            def step(s, r, first):
                act.wait_ge(m.tr, s + (NT + 1))
                if not first or r >= 2:
                    act.wait_ge(m.gu, s + (NSH - 1))
                nc.scalar.copy(blkT[:, r % 2], TR[r % 2][:, 0:DIM].rearrange(
                    "p (k n) -> p k n", k=KD)).then_inc(m.tr_sb, 1)
                gated(s + NSH, r, False)

            for r in range(RING):
                step(r, r, True)
            with act.Fori(1, later + 1) as grp:
                for r in range(RING):
                    step(grp * RING + r, r, False)
            if m.c == 0:
                act.wait_ge(s_attw, 32)
                for dst, src in WEIGHTS:
                    nc.scalar.activation(dst[0], src, ACT.Copy, scale=W_SCALE
                                         ).then_inc(a["whi"], 1)

        def attention_scalar(act):
            X, U, PJ, PT = bank[6:8], bank[4:6], bank[0:4], bank[2:4]
            act.wait_ge(s_load, 48)
            def gram_out(i):
                act.wait_ge(s_gram_mm, i + 1)
                nc.scalar.copy(gram[:, :, 1 - i, :], U[i][:, :].rearrange(
                    "p (k n) -> p k n", k=KD)).then_inc(s_gram, 1)

            gram_out(0)
            for b in range(BATCHES):
                act.wait_ge(a["var"], 2 * b + 1)
                nc.scalar.activation(a_rstd[:, TB * b:TB * (b + 1)], a_rstd[:, TB * b:TB * (b + 1)],
                                     ACT.Sqrt).then_inc(a["std"], 1)
                if b == 0:
                    gram_out(1)

                def values_out(t):
                    i = t if t < 2 else t + KC + QC
                    act.wait_ge(a["pj"], 24 * b + i + 1)
                    nc.scalar.copy(vx[:, t, :, 0:HD], PJ[i % 4][:, :].rearrange(
                        "p (g d) -> p g d", g=KVH)).then_inc(a["pj_act"], 1)

                for i in range(12):
                    if i == TB:
                        act.wait_ge(a["var"], 2 * b + 2)
                        nc.scalar.activation(a_r[:, :, :], a_r[:, :, :], ACT.Sqrt
                                             ).then_inc(a["std"], 1)
                    act.wait_ge(a["tr"], 12 * b + i + 1)
                    turned_x = (X[i % 2] if i < TB else (X + U)[(i - TB) % 4])[:, 0:DIM].rearrange(
                        "p (k n) -> p k n", k=KD)
                    if i < TB:
                        nc.scalar.copy(xnT[:, :, i * P:(i + 1) * P], turned_x
                                       ).then_inc(a["tr_sb"], 1)
                    else:
                        dst, t = (xqT, xkT)[(i - TB) % 2], (i - TB) // 2
                        nc.scalar.copy(dst[:, 0, :, t * P:(t + 1) * P], turned_x
                                       ).then_inc(a["xhi"], 1)
                    if i == TB + 3:
                        values_out(0)
                for i in range(KC + QC):
                    act.wait_ge(a["pj"], 24 * b + i + 3)
                    for half in range(2):
                        mine = slice(HD * half, HD * (half + 1))
                        if i < KC:
                            dst, w = kT[mine, 2 * i + half, 0], kn[mine, i:i + 1]
                        else:
                            dst, w = qT[mine, i - KC, half], qn[mine, i - KC:i - KC + 1]
                        ins = nc.scalar.activation(dst, PJ[(i + 2) % 4][mine, :], ACT.Copy, scale=w)
                    ins.then_inc(a["hi"], 1)
                values_out(2)
                N = PAIRS * b

                def exps(n):
                    c0 = 0 if n // 16 else P
                    if n >= 2:
                        act.wait_ge(a["pt"], N + n - 1)
                    for hh in range(2):
                        act.wait_ge(a["low"], 2 * (N + n) + hh + 1)
                        e = nc.scalar.activation(prob[:, n % 2, hh, c0:2 * P],
                                                 scores[:, n % 2, hh, c0:2 * P], ACT.Exp,
                                                 bias=low[:, n % 2, hh:hh + 1], scale=-1.0)
                    e.then_inc(a["p"], 1)

                def turned(t, i):
                    act.wait_ge(a["ot"], 16 * b + 4 * t + i + 1)
                    nc.scalar.copy(headsT[:, 0, 4 * i:4 * i + 4, :], turn_bank(t, i)[:, :].rearrange(
                        "p (c n) -> p c n", c=4)).then_inc(a["ot_sb"], 1)

                exps(0)
                exps(1)
                for n in range(PAIRS):
                    if n % 2 == 0:
                        act.wait_ge(a["pt"], N + n + 1)
                        if n >= 2:
                            act.wait_ge(a["pv"], N + n - 1)
                        k0 = 0 if n // 16 else 1
                        nc.scalar.copy(probT[:, 0, :, k0:2, :], PT[0][:, :].rearrange(
                            "p (h k q) -> p h k q", h=2, k=2)[:, :, k0:2, :]
                            ).then_inc(a["pt_act"], 1)
                    if n + 2 < PAIRS:
                        exps(n + 2)
                    if b == 0 and n < 16 and n % 4 == 3:
                        act.wait_ge(s_wo, 16 * (n // 4 + 1))
                        nc.scalar.activation(wo[:, 0, n - 3:n + 1, :], wo32, ACT.Copy,
                                             scale=W_SCALE).then_inc(a["wohi"], 1)
                    if n > 16 and n % 16 in TURN_AT:
                        turned(n // 16 - 1, TURN_AT.index(n % 16))
                for i in range(4):
                    turned(TB - 1, i)

        @block.scalar
        def _(act):
            moe_scalar(act, moe[0])
            attention_scalar(act)
            moe_scalar(act, moe[1])

        def layer_norm(v, link, tiles, var, std, n, mv, rstd, dst, norm):
            for t in tiles:
                ins = v.bn_aggr(mv[:, t, :], x_stats[:, t, :])
            link(ins)
            part = slice(tiles[0], tiles[-1] + 1)
            v.tensor_scalar(rstd[:, part], mv[:, part, 1], LN_EPS, None, ALU.add).then_inc(var, 1)
            v.wait_ge(std, n)
            link(v.reciprocal(rstd[:, part], rstd[:, part]))
            for t in tiles:
                v.tensor_scalar(dst(t), x_res[:, t, :], mv[:, t, 0:1], rstd[:, t:t + 1],
                                ALU.subtract, ALU.mult).then_inc(norm, 1)

        def residual(v, link, tt):
            v.wait_ge(a["y"], tt + 1)
            v.scalar_tensor_tensor(out=x_res[:, tt, :], in0=bank[7][:, 0:DIM],
                                   scalar=1.0 / W_SCALE, in1=x_res[:, tt, :], op0=ALU.mult,
                                   op1=ALU.add).then_inc(a["res"], 1)
            v.wait_ge(a["res"], tt + 1)
            link(v.bn_stats(x_stats[:, tt, :], x_res[:, tt, :]))

        def moe_vector(v, m):
            n = [0]

            def link(ins):
                n[0] += 1
                ins.then_inc(m.chain, 1)
                v.wait_ge(m.chain, n[0])

            for i, tiles in enumerate(LN_PARTS[m.c]):
                if m.c == 0:
                    v.wait_ge(s_x[i], 16)
                    for t in tiles:
                        ins = v.bn_stats(x_stats[:, t, :], x_res[:, t, :])
                    link(ins)
                elif i == 1:
                    residual(v, link, NT - 1)
                layer_norm(v, link, tiles, m.var, m.std, i + 1, mv, rstd,
                           lambda t: rows[:, t, 0:DIM], m.norm)
            v.wait_ge(m.logits, 1)
            logits = LOGITS[:, :].rearrange("p (t e) -> p t e", e=NE)
            link(v.tensor_reduce(rmax[:, :], logits, AX.X, ALU.max))
            v.tensor_tensor(probs[:, :, :], logits, rmax.unsqueeze(2).broadcast_to([P, NT, NE]),
                            ALU.subtract).then_inc(m.shifted, 1)
            v.wait_ge(m.expd, 1)
            for t in range(NT):
                ins = v.max(top_v[:, t, :], probs[:, t, :])
            link(ins)
            for t in range(NT):
                ins = v.max_index(top_i[:, t, :].bitcast(U32), top_v[:, t, :], probs[:, t, :])
            link(ins)
            link(v.tensor_copy(top_f[:, :, :], top_i[:, :, 0:TOPK].bitcast(U32)))
            v.wait_ge(s_const, N_CONST)
            link(v.tensor_tensor(onehot[:, :, :],
                                 iota_e[:, :].unsqueeze(1).broadcast_to([P, NT * TOPK, NE]),
                                 top_f.rearrange("p t k -> p (t k)").unsqueeze(2).broadcast_to(
                                     [P, NT * TOPK, NE]), ALU.is_equal))
            by_token = onehot.rearrange("p (t k) e -> p t k e", k=TOPK)
            link(v.tensor_tensor(pair_sum[:, :, :, :], by_token[:, :, 0:3, :],
                                 by_token[:, :, 3:6, :], ALU.add))
            link(v.tensor_tensor(sel, pair_sum[:, :, 0, :], pair_sum[:, :, 1, :], ALU.add))
            v.tensor_tensor(sel, sel, pair_sum[:, :, 2, :], ALU.add).then_inc(m.sel, 1)
            link(v.tensor_reduce(rsum[:, :], probs[:, :, :], AX.X, ALU.add))
            link(v.reciprocal(rrec[:, :], rsum[:, :]))
            link(v.tensor_reduce(wsum[:, :], top_v[:, :, 0:TOPK], AX.X, ALU.add))
            link(v.tensor_tensor(wsum[:, :], wsum[:, :], rrec[:, :], ALU.mult))
            link(v.tensor_scalar(wsum[:, :], wsum[:, :], TOPK_EPS, None, ALU.add))
            link(v.reciprocal(wrec[:, :], wsum[:, :]))
            link(v.tensor_tensor(factor[:, :], wrec[:, :], rrec[:, :], ALU.mult))
            v.wait_ge(m.sel, 1)
            link(v.scalar_tensor_tensor(out=rows[:, :, DIM:ROW], in0=probs[:, :, :], scalar=0.5,
                                        in1=sel, op0=ALU.mult, op1=ALU.mult))
            v.tensor_tensor(rows[:, :, DIM:ROW], rows[:, :, DIM:ROW],
                            factor.unsqueeze(2).broadcast_to([P, NT, NE]), ALU.mult
                            ).then_inc(m.comb, 1)
            v.wait_ge(m.rank, 1)
            link(v.tensor_tensor(more[:, :, :],
                                 COUNT[:, 0:NE].unsqueeze(2).broadcast_to([P, NE, 7]),
                                 steps_blk[:, :].unsqueeze(1).broadcast_to([P, NE, 7]),
                                 ALU.is_gt))
            link(v.tensor_reduce(extra[:, :], more[:, :, :], AX.X, ALU.add))
            link(v.tensor_tensor_scan(extra_in[:, :], ones_e[:, :], extra[:, :], 0.0, ALU.mult,
                                      ALU.add))
            link(v.tensor_tensor(base[:, :], extra_in[:, :], extra[:, :], ALU.subtract))
            link(v.tensor_scalar(base[:, :], base[:, :], float(P), float((NE - 1) * P), ALU.mult,
                                 ALU.add))
            link(v.tensor_tensor(base[:, :], base[:, :], slot0[:, :], ALU.subtract))
            rank = RANK[:, :].rearrange("p (t e) -> p t e", e=NE)
            link(v.scalar_tensor_tensor(out=pos2[:, :, :], in0=rank, scalar=float(P),
                                        in1=base.unsqueeze(1).broadcast_to([P, NT, NE]),
                                        op0=ALU.is_ge, op1=ALU.mult))
            link(v.tensor_tensor(slotm[:, :, :], rank,
                                 slot0[:, :].unsqueeze(1).broadcast_to([P, NT, NE]), ALU.add))
            link(v.tensor_tensor(slotm[:, :, :], slotm[:, :, :], pos2[:, :, :], ALU.add))
            link(v.tensor_tensor(onehot_slot.rearrange("p (t k) e -> p t k e", k=TOPK), by_token,
                                 slotm.unsqueeze(2).broadcast_to([P, NT, TOPK, NE]), ALU.mult))
            link(v.tensor_reduce(slot_f[:, :], onehot_slot[:, :, :], AX.X, ALU.add))
            link(v.tensor_copy(slot_u.bitcast(U32), slot_f[:, :]))
            v.tensor_scalar(place_u[:, 0, :].bitcast(U32), slot_u.bitcast(U32), P - 1, None,
                            ALU.bitwise_and)
            link(v.tensor_scalar(place_u[:, 1, :].bitcast(U32), slot_u.bitcast(U32), 7, None,
                                 ALU.logical_shift_right))
            link(v.tensor_copy(place_f[:, :, :], place_u.bitcast(U32)))
            link(v.tensor_scalar(owner_cmp[:, :], extra_in[:, :], iota_p[:, 0:1], 0.0, ALU.is_le,
                                 ALU.add, accum_out=owner[:, 0:1]))
            v.tensor_scalar(owner[:, 0:1], owner[:, 0:1], float(NE - 1), None, ALU.min
                            ).then_inc(m.owner, 1)
            for t in range(NT):
                ch = slice(t * TOPK, (t + 1) * TOPK)
                v.tensor_tensor(at_slot[:, ch, :],
                                iota_r[:, :].unsqueeze(1).broadcast_to([P, TOPK, P]),
                                place_f[:, 0, ch].unsqueeze(2).broadcast_to([P, TOPK, P]),
                                ALU.is_equal)
                v.tensor_tensor(at_block[:, ch, :],
                                iota_r[:, 0:MAX_BLOCKS].unsqueeze(1).broadcast_to(
                                    [P, TOPK, MAX_BLOCKS]),
                                place_f[:, 1, ch].unsqueeze(2).broadcast_to(
                                    [P, TOPK, MAX_BLOCKS]), ALU.is_equal).then_inc(m.onehots, 1)
            v.memset(slot_row[:, MAX_BLOCKS:], 0.0)
            v.wait_ge(m.ids, 1)
            link(v.tensor_scalar(slot_row[:, 0:MAX_BLOCKS].bitcast(U32),
                                 IDS[:, IDS0:IDS0 + MAX_BLOCKS], iota_p[:, 0:1], None, ALU.max))
            v.tensor_copy(gidx.bitcast(U32), slot_row[:, 0:RING].bitcast(U32)
                          ).then_inc(m.gid, RING)

            def hidden(q, r, first):
                v.wait_ge(m.silu, q + 1)
                if not first:
                    v.wait_ge(m.hT, q - 1)
                v.tensor_tensor(hid[:, r % 2, :], silu[:, r % 2, :], GU[r % 2][:, FFN:2 * FFN],
                                ALU.mult).then_inc(m.hid, 1)

            v.wait_ge(m.hT, SPLIT)
            hidden(SPLIT, SPLIT, False)
            v.wait_ge(m.ownerT, 1)
            link(v.tensor_copy(table[0:1, NE:MAX_BLOCKS].bitcast(I32),
                               OWNER[0:1, OWNER0:OWNER0 + MAX_EXTRA]))
            v.tensor_copy(table[0:1, 0:NE].bitcast(I32), iota_e[0:1, :]).then_inc(m.table, 1)
            link(v.tensor_scalar(grp_cmp[0:1, :], steps_grp[0:1, :],
                                 extra_in[0:1, NE - 1:NE], float(NE // RING - 1), ALU.is_lt, ALU.add,
                                 accum_out=grp_f[0:1, :]))
            v.tensor_copy(groups[0:1, :].bitcast(I32), grp_f[0:1, :]).then_inc(m.table, 1)

            for q in range(SPLIT + 1, NSH):
                hidden(q, q, False)

            def hidden_T(q, r, first):
                v.wait_ge(m.hT, q + 1)
                if not first:
                    v.wait_ge(m.down, q - 1)
                v.tensor_copy(hidT[0:FC, r % 2], HT[r % 2][0:FC, 0:2 * P].rearrange(
                    "p (k n) -> p k n", k=2)).then_inc(m.hT_sb, 1)

            v.wait_ge(m.table, 2)
            later = v.value_load(groups[0:1, 0:1].bitcast(I32), min_val=NE // RING - 1,
                                 max_val=MAX_BLOCKS // RING - 1)

            def keep(s, r, first):
                expert = v.value_load(table[0:1, bass.ds(s, 1)].bitcast(I32), min_val=0,
                                      max_val=NE - 1)
                v.wait_ge(m.tr, s + (NT + 1))
                if not first:
                    v.wait_ge(m.y, s - (RING - 1))
                v.tensor_copy(meta[:, r:r + 1], blk[:, r, bass.ds(expert + DIM, 1)])
                v.tensor_copy(gidx[:, r:r + 1].bitcast(U32),
                              slot_row[:, bass.ds(s + RING, 1)].bitcast(U32)).then_inc(m.gid, 1)

            def weighted(s, r, added):
                v.wait_ge(m.down, s + (NSH + 1))
                if not isinstance(added, int) or added > 0:
                    v.wait_ge(m.add[r % 2], added)
                v.tensor_copy(aidx[:, r:r + 1].bitcast(U32),
                              slot_row[:, bass.ds(s, 1)].bitcast(U32))
                v.wait_ge(m.gid, s + (RING + 1))
                v.tensor_scalar(y_sb[:, r], Y[r % 2][:, 0:DIM], meta[:, r:r + 1], None, ALU.mult
                                ).then_inc(m.y, 1)

            def step(grp, r):
                s = grp * RING + r
                first = isinstance(grp, int) and grp == 0
                if not first or r >= 1:
                    hidden_T(s + (NSH - 1), (r - 1) % RING, False)
                if not first or r >= 2:
                    weighted(s - 2, (r - 2) % RING,
                             grp * 32 - (16 if r >= 2 else 32))
                hidden(s + NSH, r, False)
                keep(s, r, first)

            for grp in range(2):
                for r in range(RING):
                    step(grp, r)
            with v.Fori(2, later + 1) as grp:
                for r in range(RING):
                    step(grp, r)
            last = later * RING + RING
            hidden_T(last + (NSH - 1), RING - 1, False)
            weighted(last - 2, RING - 2, later * 32 + 16)
            weighted(last - 1, RING - 1, later * 32 + 16)
            if m.c == 0:
                for i, (dst, src) in enumerate(WEIGHTS):
                    v.wait_ge(a["whi"], i + 1)
                    v.scalar_tensor_tensor(out=dst[1], in0=src, scalar=W_SCALE, in1=dst[0],
                                           op0=ALU.mult, op1=ALU.subtract).then_inc(a["wlo"], 1)
                v.wait_ge(s_load, 48)
                v.tensor_scalar(qn[:, :], qn[:, :], 1.0 / W_SCALE, None, ALU.mult)
                link(v.tensor_scalar(kn[:, :], kn[:, :], 1.0 / W_SCALE, None, ALU.mult))
            else:
                for i in range(NT // CHUNK):
                    sum_chunk(v, m, i)

        def sum_chunk(v, m, i):
            tiles = slice(CHUNK * i, CHUNK * (i + 1))
            v.wait_ge(m.sum_ld[i], 32)
            v.tensor_tensor(x_res[:, tiles, :], x_res[:, tiles, :], acc_b[:, tiles, :], ALU.add
                            ).then_inc(m.x, 1)
            if m.c == 0:
                v.wait_ge(m.x, i + 1)
                for t in range(CHUNK * i, CHUNK * (i + 1)):
                    ins = v.bn_stats(x_stats[:, t, :], x_res[:, t, :])
                return ins

        def attention_vector(v):
            U, PJ, SC, PT, O, X = bank[4:6], bank[0:4], bank[0:2], bank[2:4], bank[4:6], bank[6:8]
            v.wait_ge(a["wlo"], 3)
            v.memset(vx[:, :, :, HD:HD + 1], 1.0).then_inc(a["ones"], 1)
            n_chain = [0]

            def link(ins):
                n_chain[0] += 1
                ins.then_inc(a["chain"], 1)
                v.wait_ge(a["chain"], n_chain[0])

            v.wait_ge(s_load, 48)

            def normalise(b):
                layer_norm(v, link, list(range(TB * b, TB * (b + 1))), a["var"], a["std"],
                           2 * b + 1,
                           a_mv, a_rstd, lambda t: xn[:, t % TB, :], a["norm"])

            for b in range(BATCHES):
                if b == 0:
                    for i in range(NT // CHUNK // 2):
                        ins = sum_chunk(v, moe[0], i)
                    link(ins)
                    normalise(0)
                    for i in range(NT // CHUNK // 2, NT // CHUNK):
                        ins = sum_chunk(v, moe[0], i)
                    link(ins)
                else:
                    normalise(1)
                for t in range(TB):
                    v.wait_ge(a["u"], TB * b + t + 1)
                    v.wait_ge(a["norm"], TB * b + t + 1)
                    for i, width in enumerate((QD, KVD)):
                        ins = v.tensor_tensor_reduce((xq, xk)[i][:, t, :], xn[:, t, :],
                                                     U[t % 2][:, i * DIM:(i + 1) * DIM],
                                                     1.0 / width, 0.0, ALU.mult, ALU.add,
                                                     a_ss[:, t, i:i + 1])
                    ins.then_inc(a["ss"], 1)
                v.wait_ge(a["ss"], TB * (b + 1))
                v.tensor_scalar(a_r[:, :, :], a_ss[:, :, :], RMS_EPS, None, ALU.add
                                ).then_inc(a["var"], 1)
                v.wait_ge(a["std"], 2 * b + 2)
                link(v.reciprocal(a_r[:, :, :], a_r[:, :, :]))
                for t in range(TB):
                    v.tensor_scalar(xq[:, t, :], xn[:, t, :], a_r[:, t, 0:1],
                                    -float(HD) ** -0.5, ALU.mult, ALU.mult
                                    ).then_inc(a["scaled"], 1)
                    v.tensor_scalar(xk[:, t, :], xn[:, t, :], a_r[:, t, 1:2], None, ALU.mult
                                    ).then_inc(a["scaled"], 1)
                def values_out(t):
                    i = t if t < 2 else t + KC + QC
                    v.wait_ge(a["pj"], 24 * b + i + 1)
                    v.tensor_copy(vx[:, t, :, 0:HD], PJ[i % 4][:, :].rearrange(
                        "p (g d) -> p g d", g=KVH)).then_inc(a["pj_dve"], 1)

                for i in range(2 * TB):
                    dst, t = (xqT, xkT)[i % 2], i // 2
                    v.wait_ge(a["xhi"], 2 * TB * b + i + 1)
                    v.tensor_tensor(dst[:, 1, :, t * P:(t + 1) * P],
                                    (X + U)[i % 4][:, 0:DIM].rearrange("p (k n) -> p k n", k=KD),
                                    dst[:, 0, :, t * P:(t + 1) * P], ALU.subtract
                                    ).then_inc(a["xlo"], 1)
                values_out(1)
                for i in range(KC + QC):
                    v.wait_ge(a["hi"], (KC + QC) * b + i + 1)
                    if i >= KC + 4:
                        v.wait_ge(a_moved[i % 4], 8 * (KC + QC) * b + 32 * (i // 4))
                    for half in range(2):
                        mine = slice(HD * half, HD * (half + 1))
                        if i < KC:
                            hi, w = kT[mine, 2 * i + half, 0], kn[mine, i:i + 1]
                            dst = kT[mine, 2 * i + half, 1]
                        else:
                            hi, w = qT[mine, i - KC, half], qn[mine, i - KC:i - KC + 1]
                            dst = q_low[mine, i % 4]
                        ins = v.scalar_tensor_tensor(out=dst, in0=PJ[(i + 2) % 4][mine, :], scalar=w,
                                                     in1=hi, op0=ALU.mult, op1=ALU.subtract)
                    ins.then_inc(a["lo"], 1)
                values_out(3)
                N = PAIRS * b

                def biased(n):
                    t, g, pr = n // 16, n // 2 % KVH, n % 2
                    c0 = 0 if t else P
                    v.wait_ge(a["s"], N + n + 1)
                    if n >= 2:
                        v.wait_ge(a["p"], N + n - 1)
                    for hh in range(2):
                        h = REP * g + 2 * pr + hh
                        v.tensor_tensor_reduce(scores[:, n % 2, hh, c0:2 * P],
                                               nbias[:, h, c0:2 * P],
                                               SC[n % 2][:, hh * 2 * P + c0:(hh + 1) * 2 * P],
                                               1.0, 3e38, ALU.add, ALU.min,
                                               low[:, n % 2, hh:hh + 1]).then_inc(a["low"], 1)

                def turned_low(t, i):
                    v.wait_ge(a["ot_sb"], 16 * b + 4 * t + i + 1)
                    part = slice(4 * i, 4 * i + 4)
                    v.tensor_tensor(headsT[:, 1, part, :],
                                    turn_bank(t, i)[:, :].rearrange("p (c n) -> p c n", c=4),
                                    headsT[:, 0, part, :], ALU.subtract).then_inc(a["ot_lo"], 1)

                v.wait_ge(a["bias"], 1)
                biased(0)
                biased(1)
                for n in range(PAIRS + 1):
                    if n % 2 == 1:
                        v.wait_ge(a["pt"], N + n + 1)
                        if n >= 2:
                            v.wait_ge(a["pv"], N + n - 1)
                        k0 = 0 if n // 16 else 1
                        v.tensor_copy(probT[:, 1, :, k0:2, :], PT[1][:, :].rearrange(
                            "p (h k q) -> p h k q", h=2, k=2)[:, :, k0:2, :]
                            ).then_inc(a["pt_dve"], 1)
                    if n + 2 < PAIRS:
                        biased(n + 2)
                    if b == 0 and n < 16 and n % 4 == 3:
                        v.wait_ge(a["wohi"], n // 4 + 1)
                        v.scalar_tensor_tensor(out=wo[:, 1, n - 3:n + 1, :], in0=wo32,
                                               scalar=W_SCALE, in1=wo[:, 0, n - 3:n + 1, :],
                                               op0=ALU.mult, op1=ALU.subtract
                                               ).then_inc(a["wolo"], 1)
                    if n > 16 and n % 16 in LOW_AT:
                        turned_low(n // 16 - 1, LOW_AT.index(n % 16))
                    if n >= 2 and n % 2 == 0:
                        u = n // 2 - 1
                        t, g = u // KVH, u % KVH
                        v.wait_ge(a["pv"], N + n)
                        if g == 0 and t >= 2:
                            v.wait_ge(a["ot"], 16 * b + 4 * (t - 1))
                        o = O[u % 2][:, 0:REP * (HD + 1)].rearrange("p (r d) -> p r d", r=REP)
                        link(v.reciprocal(osum[:, :], o[:, :, HD]))
                        v.tensor_tensor(heads_o[:, t % 2, g * REP * HD:(g + 1) * REP * HD]
                                        .rearrange("p (r d) -> p r d", r=REP), o[:, :, 0:HD],
                                        osum.unsqueeze(2).broadcast_to([P, REP, HD]), ALU.mult
                                        ).then_inc(a["on"], 1)
                    if n == PAIRS:
                        for i in range(4):
                            turned_low(TB - 1, i)
                    if (n % 16 == OUT_AT[-1] + 1 and n > 16) or n == PAIRS:
                        if b * TB + n // 16 < NT:
                            residual(v, link, b * TB + n // 16 - 1)

        @block.vector
        def _(v):
            moe_vector(v, moe[0])
            attention_vector(v)
            moe_vector(v, moe[1])


def kernel(**inputs):
    import numpy as np
    import concourse.bacc as bacc
    from concourse.bass_utils import run_bass_kernel_spmd as run

    def f(n):
        return np.asarray(inputs[n])

    c = np.ascontiguousarray

    def by_rows(w):
        return c(w.reshape(w.shape[0] // P, P, w.shape[1]).transpose(1, 0, 2))

    wq, wk, wv, wo = (f("L0_attn_" + n) for n in ("wq", "wk", "wv", "wo"))
    order = [REP * (2 * j + half) + r for j in range(KVH // 2) for r in range(REP)
             for half in range(2)]
    wqp = wq.reshape(HEADS, HD, DIM)[order].reshape(QD, DIM)
    qnp = f("L0_attn_q_norm_w").reshape(HEADS, HD)[order].reshape(QC, P)
    gu = f("L0_ffn_w_gate_up")
    dn = f("L0_ffn_w_down")
    sgu = f("L0_ffn_ws_gate_up").reshape(2, 2, FFN, DIM).transpose(1, 0, 2, 3).reshape(
        2, 2 * FFN, DIM)
    sdn = f("L0_ffn_ws_down")
    arrays = {
        "x": c(f("L0_attn_x").reshape(TOKENS, DIM)),
        "gate": by_rows(f("L0_ffn_gate_w").T),
        "wgu": c(gu.transpose(0, 2, 1).reshape(NE, KD, P, 2 * FFN).transpose(0, 2, 1, 3)),
        "wdn": c(dn.transpose(0, 2, 1).reshape(NE, 2, FC, DIM).transpose(0, 2, 1, 3)),
        "sgu": c(sgu.transpose(0, 2, 1).reshape(2, KD, P, 2 * FFN).transpose(0, 2, 1, 3)),
        "sdn": c(sdn.T.reshape(2, 2, FC, DIM).transpose(0, 2, 1, 3)),
        "wq": by_rows(wqp.T),
        "wqn": by_rows(wq),
        "wk": by_rows(wk.T),
        "wkn": by_rows(wk),
        "wv": by_rows(wv.T),
        "wo": by_rows(wo.T),
        "qn": c(qnp.T),
        "kn": c(f("L0_attn_k_norm_w").reshape(KC, P).T),
    }
    nc = bacc.Bacc("TRN2", target_bir_lowering=False, num_devices=1)
    args = [nc.dram_tensor(f"in_{n}", v.shape, mybir.dt.from_np(v.dtype),
                           kind="ExternalInput").ap() for n, v in arrays.items()]
    args.append(nc.dram_tensor("out", (TOKENS, DIM), F32, kind="ExternalOutput").ap())
    macaron(nc, *args)
    r = run(nc, [{f"in_{n}": v for n, v in arrays.items()}], core_ids=[0])
    return r.results[0]["out"].reshape(inputs["L0_attn_x"].shape)
```
